# Optimizing a Trainium2 kernel written in Bass

```python
import numpy as np
import jax
import jax.numpy as jnp

def _softmax(x, axis=-1):
    return jax.nn.softmax(x, axis=axis)

def _gelu(x):
    return jax.nn.gelu(x, approximate=True)

def _silu(x):
    return jax.nn.silu(x)

def _sigmoid(x):
    return jax.nn.sigmoid(x)

def _layernorm(x, axis=-1, eps=1e-05):
    m = jnp.mean(x, axis=axis, keepdims=True)
    v = jnp.var(x, axis=axis, keepdims=True)
    return (x - m) / jnp.sqrt(v + eps)

def _scatter_add(tgt, idx, src, axis=0):
    return tgt.at[idx].add(src)

def _segment_sum(src, seg, n):
    return jax.ops.segment_sum(src, seg, n)
kernel_name = 'mk_hybrid_d1_jaxref_r8_09c3fc'

def setup_inputs(seed: int=0):
    np.random.seed(seed)
    _w = jnp.asarray

    def _L0_attn_a_setup():
        import jax, jax.numpy as jnp
        import numpy as np
        D_MODEL, D_STATE, D_CONV, D_INNER = (128, 16, 4, 256)
        B, S = (1, 256)
        EPS = 1e-05
        key = jax.random.key(seed)
        ks = jax.random.split(key, 8)
        sc = 0.02
        return {'x': jax.random.normal(ks[0], (B, S, D_MODEL), jnp.float32), 'ln_g': jnp.ones((D_MODEL,), jnp.float32), 'ln_b': jnp.zeros((D_MODEL,), jnp.float32), 'in_w': jax.random.normal(ks[1], (2 * D_INNER, D_MODEL), jnp.float32) * sc, 'conv_w': jax.random.normal(ks[2], (D_INNER, 1, D_CONV), jnp.float32) * sc, 'conv_b': jax.random.normal(ks[3], (D_INNER,), jnp.float32) * sc, 'xproj_w': jax.random.normal(ks[4], (2 * D_STATE + 1, D_INNER), jnp.float32) * sc, 'dt_w': jax.random.normal(ks[5], (D_INNER, 1), jnp.float32) * sc, 'dt_b': jax.random.normal(ks[6], (D_INNER,), jnp.float32) * sc, 'A_log': jnp.log(jnp.arange(1, D_STATE + 1, dtype=jnp.float32)), 'D': jnp.ones((D_INNER,), jnp.float32), 'out_w': jax.random.normal(ks[7], (D_MODEL, D_INNER), jnp.float32) * sc}
    _L0_attn_a_in = _L0_attn_a_setup()

    def _L0_attn_b_setup():
        import jax, jax.numpy as jnp
        import numpy as np
        B, N, DIM, H = (8, 512, 128, 16)
        D = DIM // H
        EPS_NORM = 1e-12
        EPS_PI = 1e-08
        key = jax.random.key(seed)
        k1, k2, k3 = jax.random.split(key, 3)
        x = jax.random.normal(k1, (B, N, DIM), dtype=jnp.float32)
        Wqkv = jax.random.normal(k2, (DIM, DIM), dtype=jnp.float32) * (1.0 / np.sqrt(DIM))
        temp = jnp.ones((H, 1), dtype=jnp.float32)
        Wout = jax.random.normal(k3, (DIM, DIM), dtype=jnp.float32) * (1.0 / np.sqrt(DIM))
        bout = jnp.zeros((DIM,), dtype=jnp.float32)
        return {'x': x, 'Wqkv': Wqkv, 'temp': temp, 'Wout': Wout, 'bout': bout}
    _L0_attn_b_in = _L0_attn_b_setup()

    def _L0_ffn_setup():
        import jax, jax.numpy as jnp
        import numpy as np
        HIDDEN = 128
        NUM_EXPERTS = 8
        TOP_K = 2
        key = jax.random.key(seed)
        k_x, k_r, k_w1, k_w2 = jax.random.split(key, 4)
        x = jax.random.normal(k_x, (4, 256, HIDDEN), dtype=jnp.float32)
        router_w = jax.random.normal(k_r, (NUM_EXPERTS, HIDDEN), dtype=jnp.float32) * HIDDEN ** (-0.5)
        w1 = jax.random.normal(k_w1, (NUM_EXPERTS, HIDDEN, 2 * HIDDEN), dtype=jnp.float32) * HIDDEN ** (-0.5)
        w2 = jax.random.normal(k_w2, (NUM_EXPERTS, 2 * HIDDEN, HIDDEN), dtype=jnp.float32) * (2 * HIDDEN) ** (-0.5)
        return {'x': x, 'router_w': router_w, 'w1': w1, 'w2': w2}
    _L0_ffn_in = _L0_ffn_setup()
    _d = {'L0_attn_a_x': _L0_attn_a_in['x'], 'L0_attn_a_ln_g': _L0_attn_a_in['ln_g'], 'L0_attn_a_ln_b': _L0_attn_a_in['ln_b'], 'L0_attn_a_in_w': _L0_attn_a_in['in_w'], 'L0_attn_a_conv_w': _L0_attn_a_in['conv_w'], 'L0_attn_a_conv_b': _L0_attn_a_in['conv_b'], 'L0_attn_a_xproj_w': _L0_attn_a_in['xproj_w'], 'L0_attn_a_dt_w': _L0_attn_a_in['dt_w'], 'L0_attn_a_dt_b': _L0_attn_a_in['dt_b'], 'L0_attn_a_A_log': _L0_attn_a_in['A_log'], 'L0_attn_a_D': _L0_attn_a_in['D'], 'L0_attn_a_out_w': _L0_attn_a_in['out_w'], 'L0_attn_b_Wqkv': _L0_attn_b_in['Wqkv'], 'L0_attn_b_temp': _L0_attn_b_in['temp'], 'L0_attn_b_Wout': _L0_attn_b_in['Wout'], 'L0_attn_b_bout': _L0_attn_b_in['bout'], 'L0_ffn_router_w': _L0_ffn_in['router_w'], 'L0_ffn_w1': _L0_ffn_in['w1'], 'L0_ffn_w2': _L0_ffn_in['w2']}
    _x0 = _d['L0_attn_a_x']
    _d['L0_attn_a_x'] = jax.random.normal(jax.random.fold_in(jax.random.key(seed), 1), (8, 1024, 128), dtype=_x0.dtype)
    del _x0
    return _d

def reference(L0_attn_a_x, L0_attn_a_ln_g, L0_attn_a_ln_b, L0_attn_a_in_w, L0_attn_a_conv_w, L0_attn_a_conv_b, L0_attn_a_xproj_w, L0_attn_a_dt_w, L0_attn_a_dt_b, L0_attn_a_A_log, L0_attn_a_D, L0_attn_a_out_w, L0_attn_b_Wqkv, L0_attn_b_temp, L0_attn_b_Wout, L0_attn_b_bout, L0_ffn_router_w, L0_ffn_w1, L0_ffn_w2):

    def _L0_attn_a_ref(x, ln_g, ln_b, in_w, conv_w, conv_b, xproj_w, dt_w, dt_b, A_log, D, out_w):
        import jax, jax.numpy as jnp
        import numpy as np
        D_MODEL, D_STATE, D_CONV, D_INNER = (128, 16, 4, 256)
        B, S = (1, 256)
        EPS = 1e-05
        b, s, _ = x.shape
        d_inner = D.shape[0]
        d_state = A_log.shape[0]
        d_conv = conv_w.shape[-1]
        residual = x
        mu = jnp.mean(x, axis=-1, keepdims=True)
        var = jnp.mean(jnp.square(x - mu), axis=-1, keepdims=True)
        xn = (x - mu) * jax.lax.rsqrt(var + EPS) * ln_g + ln_b
        xz = jnp.einsum('bsd,ed->bse', xn, in_w)
        xi, z = jnp.split(xz, 2, axis=-1)
        xc = jnp.transpose(xi, (0, 2, 1))
        xc = jnp.pad(xc, ((0, 0), (0, 0), (d_conv - 1, 0)))
        xc = jax.lax.conv_general_dilated(xc, conv_w, window_strides=(1,), padding='VALID', dimension_numbers=('NCH', 'OIH', 'NCH'), feature_group_count=d_inner)
        xc = xc + conv_b[None, :, None]
        xs = jax.nn.silu(jnp.transpose(xc, (0, 2, 1)))
        xp = jnp.einsum('bsd,ed->bse', xs, xproj_w)
        delta = jax.nn.softplus(xp[..., :1] * dt_w[:, 0] + dt_b)
        Bm = xp[..., 1:1 + d_state]
        Cm = xp[..., 1 + d_state:]
        A = -jnp.exp(A_log)
        dA = jnp.exp(delta[..., None] * A)
        dBx = delta[..., None] * Bm[:, :, None, :] * xs[..., None]

        def step(h, inp):
            dA_t, dBx_t, C_t = inp
            h = dA_t * h + dBx_t
            y_t = jnp.einsum('bdn,bn->bd', h, C_t)
            return (h, y_t)
        h0 = jnp.zeros((b, d_inner, d_state), x.dtype)
        _, ys = jax.lax.scan(step, h0, (jnp.moveaxis(dA, 1, 0), jnp.moveaxis(dBx, 1, 0), jnp.moveaxis(Cm, 1, 0)))
        y = jnp.moveaxis(ys, 0, 1) + xs * D
        y = y * jax.nn.silu(z)
        out = jnp.einsum('bse,de->bsd', y, out_w)
        return out + residual

    def _L0_attn_b_ref(x, Wqkv, temp, Wout, bout):
        import jax, jax.numpy as jnp
        import numpy as np
        B, N, DIM, H = (8, 512, 128, 16)
        D = DIM // H
        EPS_NORM = 1e-12
        EPS_PI = 1e-08
        b, n, dim = x.shape
        h, d = (H, dim // H)
        w = (x @ Wqkv.T).reshape(b, n, h, d).transpose(0, 2, 1, 3)
        norm = jnp.sqrt(jnp.sum(w * w, axis=-2, keepdims=True))
        w_normed = w / jnp.maximum(norm, EPS_NORM)
        logits = jnp.sum(w_normed * w_normed, axis=-1) * temp[None, :, :]
        Pi = jax.nn.softmax(logits, axis=1)
        Pi_norm = Pi / (jnp.sum(Pi, axis=-1, keepdims=True) + EPS_PI)
        dots = jnp.einsum('bhn,bhnd->bhd', Pi_norm, w * w)
        attn = 1.0 / (1.0 + dots)
        out = -(w * Pi[..., None]) * attn[:, :, None, :]
        out = out.transpose(0, 2, 1, 3).reshape(b, n, dim)
        return out @ Wout.T + bout

    def _L0_ffn_ref(x, router_w, w1, w2):
        import jax, jax.numpy as jnp
        import numpy as np
        HIDDEN = 128
        NUM_EXPERTS = 8
        TOP_K = 2
        bsz, seq, hidden = x.shape
        tokens = x.reshape(-1, hidden)
        logits = tokens @ router_w.T
        topk_vals, topk_idx = jax.lax.top_k(logits, TOP_K)
        weights = jax.nn.softmax(topk_vals, axis=-1)
        h = jnp.einsum('td,edf->etf', tokens, w1)
        h = jax.nn.gelu(h, approximate=False)
        out_all = jnp.einsum('etf,efd->etd', h, w2)
        out_ted = jnp.transpose(out_all, (1, 0, 2))
        gathered = jnp.take_along_axis(out_ted, topk_idx[:, :, None], axis=1)
        output = jnp.sum(weights[:, :, None] * gathered, axis=1)
        return output.reshape(bsz, seq, hidden)
    x = L0_attn_a_x
    x = x + _L0_attn_a_ref(_layernorm(x, axis=-1), L0_attn_a_ln_g, L0_attn_a_ln_b, L0_attn_a_in_w, L0_attn_a_conv_w, L0_attn_a_conv_b, L0_attn_a_xproj_w, L0_attn_a_dt_w, L0_attn_a_dt_b, L0_attn_a_A_log, L0_attn_a_D, L0_attn_a_out_w)
    x = x + _L0_ffn_ref(_layernorm(x, axis=-1), L0_ffn_router_w, L0_ffn_w1, L0_ffn_w2)
    x = x + _L0_attn_b_ref(_layernorm(x, axis=-1), L0_attn_b_Wqkv, L0_attn_b_temp, L0_attn_b_Wout, L0_attn_b_bout)
    x = x + _L0_ffn_ref(_layernorm(x, axis=-1), L0_ffn_router_w, L0_ffn_w1, L0_ffn_w2)
    return x

_drawn_inputs = setup_inputs


def setup_inputs(seed=0):
    import zlib

    import numpy as np

    out = dict(_drawn_inputs(seed))
    spreads = {'L0_attn_a_ln_g': (1.0, 0.6),
     'L0_attn_a_ln_b': (0.0, 0.8),
     'L0_attn_a_D': (1.0, 0.6),
     'L0_attn_b_temp': (1.0, 0.6),
     'L0_attn_b_bout': (0.0, 2.0)}
    factors = {'L0_attn_a_in_w': 8.0,
     'L0_attn_a_conv_w': 8.0,
     'L0_attn_a_conv_b': 8.0,
     'L0_attn_a_xproj_w': 8.0,
     'L0_attn_a_dt_w': 8.0,
     'L0_attn_a_dt_b': 8.0,
     'L0_attn_a_A_log': 8.0,
     'L0_attn_a_out_w': 8.0,
     'L0_attn_b_Wqkv': 64.0,
     'L0_attn_b_Wout': 64.0}
    for name, (base, spread) in spreads.items():
        noise = np.random.default_rng([zlib.crc32(name.encode()), seed]).standard_normal(out[name].shape)
        drawn = base * np.exp(spread * noise) if base else spread * noise
        out[name] = jnp.asarray(drawn.astype(out[name].dtype))
    for name, factor in factors.items():
        out[name] = (out[name] * factor).astype(out[name].dtype)
    return out
```

```python
from contextlib import ExitStack

import concourse.bass as bass
from concourse import mybir

F32 = mybir.dt.float32
F32R = mybir.dt.float32r
ALU = mybir.AluOpType
ACT = mybir.ActivationFunctionType
X = mybir.AxisListType.X

P = 128
BANK = 512
EPS = 1e-5
NORM2_MIN = 1e-24
PI_EPS = 1e-8
LOWEST = -3.0e38
EXP_LN = "natural_log_exp_and_others"


def hybrid_kernel(nc, x, ln_g, ln_b, in_w, conv_w, conv_b, xproj_w, dt_w, dt_b, A_log, D, out_w,
                  Wqkv, temp, Wout, bout, router_w, w1, w2, out):
    NB, T, C = x.shape
    DI = D.shape[0]
    NS = A_log.shape[0]
    TAPS = conv_w.shape[2]
    PAD = TAPS - 1
    NE, _, FF = w1.shape
    NH = temp.shape[0]
    HD = C // NH
    DH = DI // P
    FC = FF // P
    TB = T // P
    TH = T // BANK
    QB = BANK // P
    NBC = 2 * NS
    PAIRS = NS // 2
    GROUPS = NE // 2
    assert C == P and DH == 2 and FC == 2 and TH == 2 and NE == 8 and NBC == 32

    ctx = ExitStack()
    with ctx:
        def sb(name, shape, dt=F32):
            return ctx.enter_context(nc.sbuf_tensor(name, shape, dt))

        def ps(name, shape):
            return ctx.enter_context(nc.psum_tensor(name, shape, F32))

        def sem(name):
            return ctx.enter_context(nc.semaphore(name))

        ident = sb("ident", [P, P])
        sel0 = sb("sel0", [2 * NBC, NBC])
        sel = sb("sel", [2 * NBC, NBC], F32R)
        rev = sb("rev", [P, NE])
        headmask = sb("headmask", [P, NH])
        tempmask = sb("tempmask", [P, NH])
        cols = sb("cols", [P, 4 * DH + 2])
        convb, dtw, dtb, Dcol = (cols[:, i * DH:(i + 1) * DH] for i in range(4))
        gcol, bcol = cols[:, 4 * DH:4 * DH + 1], cols[:, 4 * DH + 1:4 * DH + 2]
        convw = sb("convw", [P, DH, TAPS])
        Aneg = sb("Aneg", [P, NS])
        tapw = sb("tapw", [P, TAPS, DI])
        zw = sb("zw", [P, DI])
        xpw = sb("xpw", [P, DH, 1 + NBC])
        outw = sb("outw", [P, DH, C])
        qkvw = sb("qkvw", [P, C])
        woutw = sb("woutw", [P, C])
        boutr = sb("boutr", [P, C])
        routw = sb("routw", [P, NE])
        w1s = sb("w1s", [P, NE, FF])
        w2s = sb("w2s", [P, NE, FC, C])

        xt = sb("xt", [P, TB, C])
        xn = sb("xn", [P, TB, C])
        xa = [sb(f"xa{i}", [P, TB, C]) for i in range(2)]
        xnT = sb("xnT", [P, PAD + T])
        ypost = [sb(f"ypost{i}", [P, DH, T]) for i in range(2)]
        zs = [sb(f"zs{i}", [P, DH, T]) for i in range(2)]
        delta = [sb(f"delta{i}", [P, DH, T]) for i in range(2)]
        du = [sb(f"du{i}", [P, DH, T]) for i in range(2)]
        bcs = [sb(f"bcs{i}", [2 * NBC, T], F32R) for i in range(2)]
        soft = sb("soft", [P, DH, T])
        dA = [sb(f"dA{i}", [P, DH, T]) for i in range(4)]
        hs = [sb(f"hs{i}", [P, DH, T]) for i in range(2)]
        mstat = sb("mstat", [P, TB, 6])
        mmu = sb("mmu", [P, TB])
        mvar = sb("mvar", [P, TB])
        mq = sb("mq", [P, 2, TB])
        mr = sb("mr", [P, 2, TB])
        mt = sb("mt", [P, 2, TB])

        xr = sb("xr", [P, TB, C])
        fn = sb("fn", [P, TB, C])
        fnT = sb("fnT", [P, T])
        hid = sb("hid", [P, 2, FC, T])
        wch = hid[:, 0, 0, :]
        wsq = hid[:, 0, 1, :]
        piX = hid[:, 1, 0, :]
        att = hid[:, 1, 1, :]
        fstat = sb("fstat", [P, TB, 6])
        fmu = sb("fmu", [P, TB])
        fvar = sb("fvar", [P, TB])
        fq = sb("fq", [P, TB])
        fr = sb("fr", [P, TB])
        ft = sb("ft", [P, TB])
        lg = sb("lg", [P, TB, NE])
        key = sb("key", [P, TB, NE])
        mask0 = sb("mask0", [P, TB, NE])
        mask1 = sb("mask1", [P, TB, NE])
        wt = sb("wt", [P, TB, NE])
        top = sb("top", [P, 2, TB])
        kmax = sb("kmax", [P, TB])
        gap = sb("gap", [P, TB])
        gate = sb("gate", [P, 2, TB])
        nrm = sb("nrm", [P, TH])
        nrmi = sb("nrmi", [P, 1])
        hw = sb("hw", [P, NH])
        pi = sb("pi", [P, TB, NH])
        pmx = sb("pmx", [P, TB])
        psm = sb("psm", [P, TB])
        prc = sb("prc", [P, TB])
        sPi = sb("sPi", [P, TH])
        sPw = sb("sPw", [P, TH])
        acol = sb("acol", [P, 4])

        in_raw = dA[0][:, 0, 0:512].rearrange("p (j c) -> p j c", j=4)
        tap_raw = dA[0][:, 1, :].rearrange("p (k j c) -> p k j c", k=TAPS, j=DH)
        xp_raw = dA[1][0:1 + NBC, 0, 0:DI]
        out_raw = dA[1][:, 1, 0:DI]
        qkv_raw = dA[2][:, 0, 0:C]
        wout_raw = dA[2][:, 0, C:2 * C]
        rout_raw = dA[2][0:NE, 1, 0:C]
        cols_raw = dA[2][0:4 * DH + 2, 1, P:2 * P]
        turns = ([(cols_raw, cols[:, :], 4 * DH + 2)]
                 + [(in_raw[:, DH + j, :], zw[:, j * P:(j + 1) * P], P) for j in range(DH)]
                 + [(tap_raw[:, k, j, :], tapw[:, k, j * P:(j + 1) * P], P)
                    for k in range(TAPS) for j in range(DH)]
                 + [(xp_raw[:, j * P:(j + 1) * P], xpw[:, j, :], 1 + NBC) for j in range(DH)]
                 + [(out_raw[:, j * P:(j + 1) * P], outw[:, j, :], P) for j in range(DH)]
                 + [(qkv_raw, qkvw[:, :], P), (wout_raw, woutw[:, :], P), (rout_raw, routw[:, :], NE)])

        bc_bank = [ps(f"bc_bank{i}", [P, BANK]) for i in range(3)]
        ffn_bank = [ps(f"ffn_bank{i}", [P, BANK]) for i in range(3)]
        prep_bank = ps("prep_bank", [P, BANK])
        side_bank = ps("side_bank", [P, BANK])

        w_loaded = sem("w_loaded")
        const_made = sem("const_made")
        taps_scaled = sem("taps_scaled")
        turned = sem("turned")
        turn_kept = sem("turn_kept")
        setup_act = sem("setup_act")
        setup_dve = sem("setup_dve")
        x_loaded = sem("x_loaded")
        x_used = sem("x_used")
        m_dve = sem("m_dve")
        m_act = sem("m_act")
        m_stats = sem("m_stats")
        m_rsqrt = sem("m_rsqrt")
        xn_ready = sem("xn_ready")
        x0_ready = sem("x0_ready")
        prep_full = sem("prep_full")
        prep_free = sem("prep_free")
        bc_hi = sem("bc_hi")
        bc_split = sem("bc_split")
        soft_ready = sem("soft_ready")
        pool_prep = sem("pool_prep")
        soft_one = sem("soft_one")
        delta_ready = sem("delta_ready")
        du_ready = sem("du_ready")
        yinit = sem("yinit")
        dA_ready = sem("dA_ready")
        scanned = sem("scanned")
        bc_full = sem("bc_full")
        bc_free = sem("bc_free")
        hc_added = sem("hc_added")
        gated = sem("gated")
        side_full = sem("side_full")
        side_free = sem("side_free")
        f_dve = sem("f_dve")
        f_stats = sem("f_stats")
        f_rsqrt = sem("f_rsqrt")
        fn_ready = sem("fn_ready")
        gap_ready = sem("gap_ready")
        gap_exp = sem("gap_exp")
        ffn_full = [sem(f"ffn_full{i}") for i in range(3)]
        ffn_free = [sem(f"ffn_free{i}") for i in range(3)]
        headw_ready = sem("headw_ready")
        lgt_ready = sem("lgt_ready")
        pi_exp = sem("pi_exp")
        pi_ready = sem("pi_ready")
        att_ready = sem("att_ready")
        stored = sem("stored")

        N_LOADS = 18
        M_STEPS, F_STEPS = 10, 72
        BC_USES = 2 * TH * NS
        FFN_USES = 2 * GROUPS * 4
        PREP_USES = 2 + 2 * DH * TH + TH + TH
        SIDE_USES = 2 + 3 * 2 + 2 * 1 + 2 + 1 + 2 + 2
        LN_FFN1, LN_ATT, LN_FFN2 = range(3)
        S_OUT, S_LN = 0, (2, 5, 14)
        S_ROUTE = (4, 16)
        S_QKV, S_LGT, S_PIX, S_AOUT = 7, 9, 10, 12
        assert SIDE_USES == 17

        block = ctx.enter_context(nc.Block())

        def row(ap, n):
            return ap.rearrange("(a n) -> a n", a=1).to_broadcast([P, n])

        @block.sync
        def _(sp):
            loads = [
                (in_raw, in_w.rearrange("(j p) c -> p j c", p=P)),
                (convw[:, :, :], conv_w.rearrange("(h p) a k -> p h (a k)", p=P)),
                (xp_raw, xproj_w), (out_raw, out_w), (qkv_raw, Wqkv), (wout_raw, Wout), (rout_raw, router_w),
                (cols_raw[0:DH, :], conv_b.rearrange("(h p) -> h p", p=P)),
                (cols_raw[DH:2 * DH, :], dt_w.rearrange("(h p) a -> h (p a)", p=P)),
                (cols_raw[2 * DH:3 * DH, :], dt_b.rearrange("(h p) -> h p", p=P)),
                (cols_raw[3 * DH:4 * DH, :], D.rearrange("(h p) -> h p", p=P)),
                (cols_raw[4 * DH:4 * DH + 1, :], ln_g.rearrange("(a p) -> a p", a=1)),
                (cols_raw[4 * DH + 1:4 * DH + 2, :], ln_b.rearrange("(a p) -> a p", a=1)),
                (Aneg[:, :], row(A_log, NS)), (boutr[:, :], row(bout, C)),
                (tempmask[:, :], row(temp.rearrange("h a -> (h a)"), NH)),
                (w1s[:, :, :], w1.rearrange("e c f -> c e f")),
                (w2s[:, :, :, :], w2.rearrange("e (j f) c -> f e j c", f=P)),
            ]
            assert len(loads) == N_LOADS
            sp.sem_inc(stored, 16)
            sp.dma_start(xt[:, :, :], x[0].rearrange("(b p) c -> p b c", p=P)).then_inc(x_loaded, 16)
            for dst, src in loads:
                sp.dma_start(dst, src).then_inc(w_loaded, 16)
            with sp.Fori(1, NB) as b:
                sp.wait_ge(x_used, b)
                sp.dma_start(xt[:, :, :], x[b].rearrange("(b p) c -> p b c", p=P)).then_inc(x_loaded, 16)
                for w in range(3):
                    sp.wait_ge(ffn_free[w], 1 + FFN_USES * b)
                sp.dma_start(out[b - 1].rearrange("(b p) c -> p b c", p=P), xr[:, :, :]).then_inc(stored, 16)
            for w in range(3):
                sp.wait_ge(ffn_free[w], 1 + FFN_USES * NB)
            sp.dma_start(out[NB - 1].rearrange("(b p) c -> p b c", p=P), xr[:, :, :]).then_inc(stored, 16)
            sp.wait_ge(stored, 16 + 16 * NB)

        @block.gpsimd
        def _(pool):
            nc.gpsimd.memset(ident[:, :], 0.0)
            nc.gpsimd.memset(sel0[:, :], 0.0)
            nc.gpsimd.memset(headmask[:, :], 1.0)
            nc.gpsimd.memset(xnT[:, 0:PAD], 0.0)
            nc.gpsimd.iota(rev[:, :], pattern=[[-1, NE]], base=NE, channel_multiplier=0,
                           allow_small_or_imprecise_dtypes=True).then_inc(const_made, 1)
            pool.wait_ge(const_made, 1)
            nc.gpsimd.affine_select(out=ident[:, :], in_=ident[:, :], compare_op=ALU.not_equal, fill=1.0,
                                    base=0, pattern=[[-1, P]], channel_multiplier=1)
            nc.gpsimd.affine_select(out=sel0[:, :], in_=sel0[:, :], compare_op=ALU.not_equal, fill=1.0,
                                    base=0, pattern=[[-1, NBC]], channel_multiplier=1).then_inc(const_made, 1)
            pool.wait_ge(const_made, 2)
            nc.gpsimd.affine_select(out=sel0[:, :], in_=sel0[:, :], compare_op=ALU.not_equal, fill=1.0,
                                    base=-NBC, pattern=[[-1, NBC]], channel_multiplier=1)
            nc.gpsimd.affine_select(out=headmask[:, :], in_=headmask[:, :], compare_op=ALU.is_ge, fill=0.0,
                                    base=0, pattern=[[-HD, NH]], channel_multiplier=1).then_inc(const_made, 1)
            pool.wait_ge(const_made, 3)
            nc.gpsimd.affine_select(out=headmask[:, :], in_=headmask[:, :], compare_op=ALU.is_ge, fill=0.0,
                                    base=HD - 1, pattern=[[HD, NH]], channel_multiplier=-1).then_inc(const_made, 1)

            def prep(b, q):
                pool.wait_ge(x0_ready, b + 1)
                nc.gpsimd.tensor_tensor(xa[q][:, :, :], xa[q][:, :, :], xt[:, :, :], ALU.add).then_inc(x_used, 1)
                pool.wait_ge(soft_ready, b + 1)
                nc.gpsimd.tensor_tensor(delta[q][:, :, :], delta[q][:, :, :], du[q][:, :, :], ALU.add).then_inc(pool_prep, 1)
                pool.wait_ge(soft_one, b + 1)
                nc.gpsimd.tensor_tensor(soft[:, :, :], soft[:, :, :], du[q][:, :, :], ALU.subtract).then_inc(pool_prep, 1)
                pool.wait_ge(pool_prep, 2 * b + 2)
                nc.gpsimd.tensor_tensor(delta[q][:, :, :], delta[q][:, :, :], soft[:, :, :], ALU.add).then_inc(delta_ready, 1)

            def sum_states(b, q, n):
                if n == 0:
                    pool.wait_ge(yinit, b + 1)
                pool.wait_ge(bc_free, 1 + BC_USES * b + 2 * TH * (n + 1))
                pool.wait_ge(hc_added, 1 + NS * b + n)
                nc.gpsimd.tensor_tensor(ypost[q][:, :, :], ypost[q][:, :, :], hs[n % 2][:, :, :], ALU.add).then_inc(hc_added, 1)

            with pool.Fori(0, NB // 2) as bb:
                for q in range(2):
                    b = bb * 2 + q
                    prep(b, q)
                    for n in range(NS):
                        sum_states(b, q, n)

        @block.scalar
        def _(act):
            act.wait_ge(w_loaded, 16 * N_LOADS)
            nc.scalar.preload_act_table_set(EXP_LN)
            nc.scalar.activation(Aneg[:, :], Aneg[:, :], ACT.Exp).then_inc(setup_act, 1)
            act.wait_ge(setup_act, 1)
            nc.scalar.mul(Aneg[:, :], Aneg[:, :], -1.0).then_inc(setup_act, 1)

            def rsqrt(dst, src, before, done, b, k, per):
                act.wait_ge(before, b + k if per == 1 else b * per + k)
                nc.scalar.activation(dst, src, ACT.Ln).then_inc(done, 1)
                act.wait_ge(done, (b * per + k) * 2 - 1)
                nc.scalar.activation(dst, dst, ACT.Exp, scale=-0.5).then_inc(done, 1)

            def prep_norm(b, q):
                nc.scalar.preload_act_table_set(EXP_LN)
                rsqrt(mr[:, :, :], mq[:, :, :], m_stats, m_rsqrt, b, 1, 1)
                for th in range(TH):
                    act.wait_ge(prep_full, PREP_USES * b + th + 1)
                    nc.scalar.activation(xnT[:, PAD + th * BANK:PAD + (th + 1) * BANK], prep_bank[:, :],
                                         ACT.Identity, scale=gcol[:, 0:1], bias=bcol[:, 0:1]).then_inc(prep_free, 1)

            def prep_silu(b, q):
                nc.scalar.preload_act_table(ACT.Silu)
                for k in range(2 * DH * TH):
                    dh, th = k // TH % DH, k % TH
                    act.wait_ge(prep_full, PREP_USES * b + TH + k + 1)
                    dst = (zs if k < DH * TH else ypost)[q][:, dh, th * BANK:(th + 1) * BANK]
                    if k < DH * TH:
                        nc.scalar.activation(dst, prep_bank[:, :], ACT.Silu).then_inc(prep_free, 1)
                    else:
                        nc.scalar.activation(dst, prep_bank[:, :], ACT.Silu, bias=convb[:, dh:dh + 1]).then_inc(prep_free, 1)

            def prep_soft(b, q):
                nc.scalar.preload_act_table_set(EXP_LN)
                u0 = TH + 2 * DH * TH
                for th in range(TH):
                    cols = slice(th * BANK, (th + 1) * BANK)
                    act.wait_ge(prep_full, PREP_USES * b + u0 + th + 1)
                    nc.scalar.activation(bcs[q][0:NBC, cols], prep_bank[0:NBC, :], ACT.Copy).then_inc(bc_hi, 1)
                for th in range(TH):
                    cols = slice(th * BANK, (th + 1) * BANK)
                    act.wait_ge(prep_full, PREP_USES * b + u0 + TH + th + 1)
                    for dh in range(DH):
                        nc.scalar.activation(soft[:, dh, cols], prep_bank[:, :], ACT.Abs,
                                             scale=dtw[:, dh:dh + 1], bias=dtb[:, dh:dh + 1])
                        last = nc.scalar.activation(delta[q][:, dh, cols], prep_bank[:, :], ACT.Relu,
                                                    scale=dtw[:, dh:dh + 1], bias=dtb[:, dh:dh + 1])
                    last.then_inc(prep_free, 1)
                act.wait_ge(prep_free, 1 + PREP_USES * (b + 1))
                nc.scalar.activation(soft[:, :, :], soft[:, :, :], ACT.Exp, scale=-1.0).then_inc(m_act, 1)
                act.wait_ge(m_act, b + 1)
                nc.scalar.activation(du[q][:, :, :], soft[:, :, :], ACT.Ln, bias=1.0).then_inc(soft_ready, 1)

            def prep_end(b, q):
                act.wait_ge(du_ready, b + 1)
                for dh in range(DH):
                    last = nc.scalar.activation(ypost[q][:, dh, :], ypost[q][:, dh, :], ACT.Copy, scale=Dcol[:, dh:dh + 1])
                last.then_inc(yinit, 1)

            def decay(b, q, n):
                if n == 0:
                    act.wait_ge(delta_ready, b + 1)
                j = NS * b + n
                if n >= 4:
                    act.wait_ge(scanned, j - 3)
                nc.scalar.activation(dA[n % 4][:, :, :], delta[q][:, :, :], ACT.Exp, scale=Aneg[:, n:n + 1]).then_inc(dA_ready, 1)

            def norm_rsqrt(b, k):
                nc.scalar.preload_act_table_set(EXP_LN)
                rsqrt(fr[:, :], fq[:, :], f_stats, f_rsqrt, b, k + 1, 3)

            def norm_turned(b, k):
                for th in range(TH):
                    act.wait_ge(side_full, SIDE_USES * b + S_LN[k] + th + 1)
                    nc.scalar.activation(fnT[:, th * BANK:(th + 1) * BANK], side_bank[:, :], ACT.Copy).then_inc(side_free, 1)

            def route(b, f):
                act.wait_ge(gap_ready, 2 * b + f + 1)
                nc.scalar.activation(gap[:, :], gap[:, :], ACT.Exp).then_inc(gap_exp, 1)

            def gelus(b, f, g):
                nc.scalar.preload_act_table(ACT.Gelu)
                G = (b * 2 + f) * GROUPS + g
                for u in range(2 * TH * FC):
                    e, th, fc = u // (TH * FC), u // FC % TH, u % FC
                    act.wait_ge(ffn_full[u % 3], 4 * G + u // 3 + 1)
                    nc.scalar.activation(hid[:, e, fc, th * BANK:(th + 1) * BANK], ffn_bank[u % 3][:, :],
                                         ACT.Gelu).then_inc(ffn_free[u % 3], 1)

            def attend(b):
                for th in range(TH):
                    cols = slice(th * BANK, (th + 1) * BANK)
                    act.wait_ge(side_full, SIDE_USES * b + S_QKV + th + 1)
                    nc.scalar.activation(wch[:, cols], side_bank[:, :], ACT.Copy)
                    nc.scalar.activation(wsq[:, cols], side_bank[:, :], ACT.Square,
                                         accum_out=nrm[:, th:th + 1]).then_inc(side_free, 1)
                act.wait_ge(lgt_ready, b + 1)
                nc.scalar.activation(pi[:, :, :], pi[:, :, :], ACT.Exp).then_inc(pi_exp, 1)
                for th in range(TH):
                    act.wait_ge(side_full, SIDE_USES * b + S_PIX + th + 1)
                    nc.scalar.activation(piX[:, th * BANK:(th + 1) * BANK], side_bank[:, :], ACT.Copy,
                                         accum_out=sPi[:, th:th + 1]).then_inc(side_free, 1)

            with act.Fori(0, NB // 2) as bb:
                for q in range(2):
                    b = bb * 2 + q
                    prep_norm(b, q)
                    prep_silu(b, q)
                    prep_soft(b, q)
                    prep_end(b, q)
                    for n in range(NS):
                        decay(b, q, n)
                    for f in range(2):
                        k = (LN_FFN1, LN_FFN2)[f]
                        norm_rsqrt(b, k)
                        norm_turned(b, k)
                        route(b, f)
                        for g in range(GROUPS):
                            gelus(b, f, g)
                        if f == 0:
                            norm_rsqrt(b, LN_ATT)
                            norm_turned(b, LN_ATT)
                            attend(b)

        @block.vector
        def _(dve):
            for start in [prep_free, bc_free, side_free, hc_added] + ffn_free:
                nc.vector.sem_inc(start, 1)
            dve.wait_ge(const_made, 4)
            nc.vector.tensor_copy(sel[:, :], sel0[:, :]).then_inc(setup_dve, 1)
            dve.wait_ge(w_loaded, 16 * N_LOADS)
            nc.vector.tensor_tensor(tempmask[:, :], tempmask[:, :], headmask[:, :], ALU.mult).then_inc(setup_dve, 1)
            for k in range(TAPS):
                for j in range(DH):
                    last = nc.vector.tensor_scalar(tap_raw[:, k, j, :], in_raw[:, j, :], convw[:, j, k:k + 1],
                                                   None, ALU.mult)
            last.then_inc(taps_scaled, 1)
            for i, (_, dst, _) in enumerate(turns):
                dve.wait_ge(turned, i + 1)
                nc.vector.tensor_copy(dst, bc_bank[i % 3][:, 0:dst.shape[-1]]).then_inc(turn_kept, 1)

            class Chain:

                def __init__(self, s, base):
                    self.s, self.base, self.n = s, base, 0

                def __call__(self, ins):
                    self.n += 1
                    ins.then_inc(self.s, 1)
                    dve.wait_ge(self.s, self.base + self.n)

            def newton(step, r, q, t):
                step(nc.vector.tensor_tensor(t, r, r, ALU.mult))
                step(nc.vector.tensor_tensor(t, t, q, ALU.mult))
                step(nc.vector.tensor_scalar(t, t, -0.5, 1.5, ALU.mult, ALU.add))
                step(nc.vector.tensor_tensor(r, r, t, ALU.mult))

            def stats(step, src, stat, mu, var, t):
                for tb in range(TB):
                    last = nc.vector.bn_stats(stat[:, tb, :], src[:, tb, :])
                step(last)
                nc.vector.tensor_tensor(mu, stat[:, :, 1], stat[:, :, 4], ALU.add)
                step(nc.vector.tensor_tensor(t, stat[:, :, 1], stat[:, :, 4], ALU.subtract))
                nc.vector.tensor_tensor(var, stat[:, :, 2], stat[:, :, 5], ALU.add)
                step(nc.vector.tensor_tensor(t, t, t, ALU.mult))
                nc.vector.tensor_scalar(mu, mu, 0.5, None, ALU.mult)
                step(nc.vector.scalar_tensor_tensor(out=var, in0=t, scalar=C / 4.0, in1=var, op0=ALU.mult, op1=ALU.add))

            def prep_norm(b, q):
                step = Chain(m_dve, b * M_STEPS)
                dve.wait_ge(x_loaded, 16 * (b + 1))
                stats(step, xt, mstat, mmu[:, :], mvar[:, :], mt[:, 0, :])
                var = mvar[:, :]
                step(nc.vector.tensor_scalar(var, var, 1.0 / C, None, ALU.mult))
                step(nc.vector.tensor_scalar(mq[:, 0, :], var, EPS, None, ALU.add))
                nc.vector.scalar_tensor_tensor(out=mq[:, 1, :], in0=mq[:, 0, :], scalar=EPS, in1=var,
                                               op0=ALU.mult, op1=ALU.add).then_inc(m_stats, 1)
                dve.wait_ge(m_rsqrt, 2 * (b + 1))
                newton(step, mr[:, :, :], mq[:, :, :], mt[:, :, :])
                for tb in range(TB):
                    last = nc.vector.tensor_scalar(xn[:, tb, :], xt[:, tb, :], mmu[:, tb:tb + 1], mr[:, 1, tb:tb + 1],
                                                   ALU.subtract, ALU.mult)
                last.then_inc(xn_ready, 1)
                for tb in range(TB):
                    last = nc.vector.tensor_scalar(xa[q][:, tb, :], xt[:, tb, :], mmu[:, tb:tb + 1], mr[:, 0, tb:tb + 1],
                                                   ALU.subtract, ALU.mult)
                last.then_inc(x0_ready, 1)

            def prep_split(b, q):
                u0 = TH + 2 * DH * TH
                for th in range(TH):
                    cols = slice(th * BANK, (th + 1) * BANK)
                    dve.wait_ge(bc_hi, TH * b + th + 1)
                    nc.vector.tensor_tensor(bcs[q][NBC:2 * NBC, cols], prep_bank[0:NBC, :],
                                            bcs[q][0:NBC, cols].bitcast(F32), ALU.subtract).then_inc(prep_free, 1)

            def prep_one(b, q):
                dve.wait_ge(pool_prep, 2 * b + 1)
                nc.vector.tensor_scalar(du[q][:, :, :], soft[:, :, :], 1.0, -1.0, ALU.add, ALU.add).then_inc(soft_one, 1)

            def prep_du(b, q):
                dve.wait_ge(delta_ready, b + 1)
                nc.vector.tensor_tensor(du[q][:, :, :], delta[q][:, :, :], ypost[q][:, :, :], ALU.mult).then_inc(du_ready, 1)
                dve.wait_ge(du_ready, b + 1)

            def state(b, q, n):
                j = NS * b + n
                h = hs[n % 2]
                if n >= 2:
                    dve.wait_ge(hc_added, 1 + j - 1)
                for th in range(TH):
                    cols = slice(th * BANK, (th + 1) * BANK)
                    u = 2 * TH * j + th
                    dve.wait_ge(bc_full, u + 1)
                    last = nc.vector.tensor_tensor(
                        h[:, :, cols], du[q][:, :, cols],
                        bc_bank[(2 * TH * n + th ) % 3][:, :].unsqueeze(1).to_broadcast([P, DH, BANK]), ALU.mult)
                    last.then_inc(bc_free, 1)
                dve.wait_ge(bc_free, 1 + 2 * TH * j + TH)
                dve.wait_ge(dA_ready, j + 1)
                for dh in range(DH):
                    last = nc.vector.tensor_tensor_scan(h[:, dh, :], dA[n % 4][:, dh, :], h[:, dh, :], 0.0,
                                                        ALU.mult, ALU.add)
                last.then_inc(scanned, 1)
                dve.wait_ge(scanned, j + 1)
                for th in range(TH):
                    cols = slice(th * BANK, (th + 1) * BANK)
                    dve.wait_ge(bc_full, 2 * TH * j + TH + th + 1)
                    nc.vector.tensor_tensor(
                        h[:, :, cols], h[:, :, cols],
                        bc_bank[(2 * TH * n + TH + th ) % 3][:, :].unsqueeze(1).to_broadcast([P, DH, BANK]),
                        ALU.mult).then_inc(bc_free, 1)

            def gate_y(b, q):
                dve.wait_ge(hc_added, 1 + NS * (b + 1))
                nc.vector.tensor_tensor(ypost[q][:, :, :], ypost[q][:, :, :], zs[q][:, :, :], ALU.mult).then_inc(gated, 1)

            def residual(b, q):
                if True:
                    dve.wait_ge(stored, 16 + 16 * b)
                for th in range(TH):
                    dve.wait_ge(side_full, SIDE_USES * b + S_OUT + th + 1)
                    rows = slice(th * QB, (th + 1) * QB)
                    nc.vector.tensor_tensor(xr[:, rows, :], xa[q][:, rows, :],
                                            side_bank[:, :].rearrange("p (b c) -> p b c", c=C), ALU.add).then_inc(side_free, 1)
                dve.wait_ge(side_free, 1 + SIDE_USES * b + S_OUT + TH)

            def norm(step, b, k):
                stats(step, xr, fstat, fmu[:, :], fvar[:, :], ft[:, :])
                nc.vector.tensor_scalar(fq[:, :], fvar[:, :], 1.0 / C, EPS, ALU.mult, ALU.add).then_inc(f_stats, 1)
                dve.wait_ge(f_rsqrt, 2 * (3 * b + k + 1))
                newton(step, fr[:, :], fq[:, :], ft[:, :])
                for tb in range(TB):
                    last = nc.vector.tensor_scalar(fn[:, tb, :], xr[:, tb, :], fmu[:, tb:tb + 1], fr[:, tb:tb + 1],
                                                   ALU.subtract, ALU.mult)
                last.then_inc(fn_ready, 1)

            def wide(ap):
                return ap.unsqueeze(2).to_broadcast([P, TB, NE])

            def route(step, b, f):
                dve.wait_ge(side_full, SIDE_USES * b + S_ROUTE[f] + 1)
                nc.vector.tensor_copy(lg[:, :, :], side_bank[:, 0:TB * NE].rearrange("p (b e) -> p b e", e=NE)).then_inc(side_free, 1)
                dve.wait_ge(side_free, 1 + SIDE_USES * b + S_ROUTE[f] + 1)
                for i, m in enumerate((mask0, mask1)):
                    step(nc.vector.tensor_reduce(top[:, i, :], lg[:, :, :], X, ALU.max))
                    step(nc.vector.tensor_tensor(key[:, :, :], lg[:, :, :], wide(top[:, i, :]), ALU.is_equal))
                    step(nc.vector.tensor_tensor(key[:, :, :], key[:, :, :],
                                                 rev[:, :].unsqueeze(1).to_broadcast([P, TB, NE]), ALU.mult))
                    step(nc.vector.tensor_reduce(kmax[:, :], key[:, :, :], X, ALU.max))
                    step(nc.vector.tensor_tensor(m[:, :, :], key[:, :, :], wide(kmax[:, :]), ALU.is_equal))
                    if i == 0:
                        step(nc.vector.scalar_tensor_tensor(out=lg[:, :, :], in0=m[:, :, :], scalar=LOWEST,
                                                            in1=lg[:, :, :], op0=ALU.mult, op1=ALU.add))
                nc.vector.tensor_tensor(gap[:, :], top[:, 1, :], top[:, 0, :], ALU.subtract).then_inc(gap_ready, 1)
                dve.wait_ge(gap_exp, 2 * b + f + 1)
                step(nc.vector.tensor_scalar(gate[:, 1, :], gap[:, :], 1.0, None, ALU.add))
                step(nc.vector.reciprocal(gate[:, 0, :], gate[:, 1, :]))
                step(nc.vector.tensor_tensor(gate[:, 1, :], gap[:, :], gate[:, 0, :], ALU.mult))
                nc.vector.tensor_tensor(mask0[:, :, :], mask0[:, :, :], wide(gate[:, 0, :]), ALU.mult)
                step(nc.vector.tensor_tensor(mask1[:, :, :], mask1[:, :, :], wide(gate[:, 1, :]), ALU.mult))
                step(nc.vector.tensor_tensor(wt[:, :, :], mask0[:, :, :], mask1[:, :, :], ALU.add))

            def add_experts(b, f, g, last_step):
                G = (b * 2 + f) * GROUPS + g
                for v in range(2 * TH):
                    e, th = v // TH, v % TH
                    u = 2 * TH * FC + v
                    dve.wait_ge(ffn_full[u % 3], 4 * G + u // 3 + 1)
                    if v >= TH:
                        dve.wait_ge(ffn_free[(u - TH) % 3], 1 + 4 * G + (u - TH) // 3 + 1)
                    elif g:
                        dve.wait_ge(ffn_free[(u + TH) % 3], 1 + 4 * (G - 1) + (u + TH) // 3 + 1)
                    for i in range(QB):
                        tb = th * QB + i
                        last = nc.vector.scalar_tensor_tensor(
                            out=xr[:, tb, :], in0=ffn_bank[u % 3][:, i * C:(i + 1) * C],
                            scalar=wt[:, tb, 2 * g + e:2 * g + e + 1], in1=xr[:, tb, :], op0=ALU.mult, op1=ALU.add)
                    last.then_inc(ffn_free[u % 3], 1)
                if last_step:
                    for w in range(3):
                        dve.wait_ge(ffn_free[w], 1 + 4 * (G + 1))

            def attend(step, b):
                dve.wait_ge(side_free, 1 + SIDE_USES * b + S_QKV + TH)
                step(nc.vector.tensor_tensor(nrmi[:, :], nrm[:, 0:1], nrm[:, 1:2], ALU.add))
                step(nc.vector.tensor_scalar(nrmi[:, :], nrmi[:, :], NORM2_MIN, None, ALU.max))
                step(nc.vector.reciprocal(nrmi[:, :], nrmi[:, :]))
                nc.vector.tensor_scalar(hw[:, :], tempmask[:, :], nrmi[:, 0:1], None, ALU.mult).then_inc(headw_ready, 1)
                dve.wait_ge(side_full, SIDE_USES * b + S_LGT + 1)
                nc.vector.tensor_copy(pi[:, :, :], side_bank[:, 0:TB * NH].rearrange("p (b h) -> p b h", h=NH)).then_inc(side_free, 1)
                dve.wait_ge(side_free, 1 + SIDE_USES * b + S_LGT + 1)
                step(nc.vector.tensor_reduce(pmx[:, :], pi[:, :, :], X, ALU.max))
                nc.vector.tensor_tensor(pi[:, :, :], pi[:, :, :], pmx[:, :].unsqueeze(2).to_broadcast([P, TB, NH]),
                                        ALU.subtract).then_inc(lgt_ready, 1)
                dve.wait_ge(pi_exp, b + 1)
                step(nc.vector.tensor_reduce(psm[:, :], pi[:, :, :], X, ALU.add))
                step(nc.vector.reciprocal(prc[:, :], psm[:, :]))
                nc.vector.tensor_tensor(fn[:, :, :].rearrange("p b (h d) -> p b h d", d=HD),
                                        pi[:, :, :].unsqueeze(3).to_broadcast([P, TB, NH, HD]),
                                        prc[:, :].unsqueeze(2).unsqueeze(3).to_broadcast([P, TB, NH, HD]),
                                        ALU.mult).then_inc(pi_ready, 1)
                dve.wait_ge(side_free, 1 + SIDE_USES * b + S_PIX + TH)
                for th in range(TH):
                    cols = slice(th * BANK, (th + 1) * BANK)
                    step(nc.vector.scalar_tensor_tensor(out=att[:, cols], in0=piX[:, cols], scalar=1.0, in1=wsq[:, cols],
                                                        op0=ALU.mult, op1=ALU.mult, accum_out=sPw[:, th:th + 1]))
                step(nc.vector.tensor_tensor(acol[:, 0:1], sPi[:, 0:1], sPi[:, 1:2], ALU.add))
                step(nc.vector.tensor_scalar(acol[:, 0:1], acol[:, 0:1], PI_EPS, None, ALU.add))
                step(nc.vector.reciprocal(acol[:, 1:2], acol[:, 0:1]))
                step(nc.vector.tensor_tensor(acol[:, 2:3], sPw[:, 0:1], sPw[:, 1:2], ALU.add))
                step(nc.vector.tensor_tensor(acol[:, 2:3], acol[:, 2:3], acol[:, 1:2], ALU.mult))
                step(nc.vector.tensor_scalar(acol[:, 2:3], acol[:, 2:3], 1.0, -1.0, ALU.add, ALU.mult))
                step(nc.vector.reciprocal(acol[:, 3:4], acol[:, 2:3]))
                nc.vector.scalar_tensor_tensor(out=att[:, :], in0=wch[:, :], scalar=acol[:, 3:4], in1=piX[:, :],
                                               op0=ALU.mult, op1=ALU.mult).then_inc(att_ready, 1)
                step(nc.vector.tensor_tensor(xr[:, :, :], xr[:, :, :], boutr[:, :].unsqueeze(1).to_broadcast([P, TB, C]),
                                             ALU.add))
                for th in range(TH):
                    rows = slice(th * QB, (th + 1) * QB)
                    dve.wait_ge(side_full, SIDE_USES * b + S_AOUT + th + 1)
                    nc.vector.tensor_tensor(xr[:, rows, :], xr[:, rows, :],
                                            side_bank[:, :].rearrange("p (b c) -> p b c", c=C), ALU.add).then_inc(side_free, 1)
                dve.wait_ge(side_free, 1 + SIDE_USES * b + S_AOUT + TH)

            with dve.Fori(0, NB // 2) as bb:
                for q in range(2):
                    b = bb * 2 + q
                    prep_norm(b, q)
                    prep_split(b, q)
                    prep_one(b, q)
                    prep_du(b, q)
                    for n in range(NS):
                        state(b, q, n)
                    gate_y(b, q)
                    residual(b, q)
                    step = Chain(f_dve, b * F_STEPS)
                    for f in range(2):
                        norm(step, b, (LN_FFN1, LN_FFN2)[f])
                        route(step, b, f)
                        for g in range(GROUPS):
                            add_experts(b, f, g, g == GROUPS - 1)
                        if f == 0:
                            norm(step, b, LN_ATT)
                            attend(step, b)
                    assert step.n == F_STEPS, step.n

        @block.tensor
        def _(pe):
            pe.wait_ge(const_made, 4)
            pe.wait_ge(w_loaded, 16 * N_LOADS)
            pe.wait_ge(taps_scaled, 1)
            for i, (src, dst, n) in enumerate(turns):
                if i >= 3:
                    pe.wait_ge(turn_kept, i - 2)
                nc.tensor.transpose(bc_bank[i % 3][:, 0:n], src, ident[0:n, 0:n]).then_inc(turned, 1)
            pe.wait_ge(turn_kept, len(turns))
            pe.wait_ge(setup_dve, 2)

            def prep_slot(b, u):
                pe.wait_ge(prep_free, 1 + PREP_USES * b + u)

            def prep(b, q):
                pe.wait_ge(xn_ready, b + 1)
                for th in range(TH):
                    prep_slot(b, th)
                    for i in range(QB):
                        last = nc.tensor.transpose(prep_bank[:, i * P:(i + 1) * P], xn[:, th * QB + i, :], ident[:, :])
                    last.then_inc(prep_full, 1)
                for k in range(2 * DH * TH):
                    dh, th = k // TH % DH, k % TH
                    prep_slot(b, TH + k)
                    if k < DH * TH:
                        last = nc.tensor.matmul(prep_bank[:, :], zw[:, dh * P:(dh + 1) * P],
                                                xnT[:, PAD + th * BANK:PAD + (th + 1) * BANK], start=True, stop=True)
                    else:
                        for tap in range(TAPS):
                            last = nc.tensor.matmul(prep_bank[:, :], tapw[:, tap, dh * P:(dh + 1) * P],
                                                    xnT[:, th * BANK + tap:th * BANK + tap + BANK],
                                                    start=(tap == 0), stop=(tap == TAPS - 1))
                    last.then_inc(prep_full, 1)
                for k in range(2 * TH):
                    th = k % TH
                    prep_slot(b, TH + 2 * DH * TH + k)
                    for dh in range(DH):
                        w = xpw[:, dh, 1:1 + NBC] if k < TH else xpw[:, dh, 0:1].to_broadcast([P, P])
                        last = nc.tensor.matmul(prep_bank[0:w.shape[1], :], w, ypost[q][:, dh, th * BANK:(th + 1) * BANK],
                                                start=(dh == 0), stop=(dh == DH - 1))
                    last.then_inc(prep_full, 1)

            def spread(b, q, n):
                for k in range(2 * TH):
                    th, j = k % TH, (n if k < TH else NS + n)
                    u = 2 * TH * n + k
                    pe.wait_ge(bc_free, 1 + BC_USES * b + max(u - 2, 0))
                    nc.tensor.matmul(bc_bank[u % 3][:, :], sel[:, j:j + 1].to_broadcast([2 * NBC, P]),
                                     bcs[q][:, th * BANK:(th + 1) * BANK], start=True, stop=True).then_inc(bc_full, 1)

            def side_slot(b, s):
                pe.wait_ge(side_free, 1 + SIDE_USES * b + s)

            def project(b, q):
                pe.wait_ge(gated, b + 1)
                for th in range(TH):
                    side_slot(b, S_OUT + th)
                    for i in range(QB):
                        tok = slice((th * QB + i) * P, (th * QB + i + 1) * P)
                        for dh in range(DH):
                            last = nc.tensor.matmul(side_bank[:, i * C:(i + 1) * C], ypost[q][:, dh, tok], outw[:, dh, :],
                                                    start=(dh == 0), stop=(dh == DH - 1))
                    last.then_inc(side_full, 1)

            def turn_normed(b, k):
                pe.wait_ge(fn_ready, 3 * b + k + 1)
                for th in range(TH):
                    side_slot(b, S_LN[k] + th)
                    for i in range(QB):
                        last = nc.tensor.transpose(side_bank[:, i * P:(i + 1) * P], fn[:, th * QB + i, :], ident[:, :])
                    last.then_inc(side_full, 1)
                pe.wait_ge(side_free, 1 + SIDE_USES * b + S_LN[k] + TH)

            def logits(b, f):
                side_slot(b, S_ROUTE[f])
                for tb in range(TB):
                    last = nc.tensor.matmul(side_bank[:, tb * NE:(tb + 1) * NE], fnT[:, tb * P:(tb + 1) * P], routw[:, :],
                                            start=True, stop=True)
                last.then_inc(side_full, 1)

            def freed(G, u):
                pe.wait_ge(ffn_free[u % 3], 1 + 4 * G + u // 3 + 1)

            def experts_in(b, f, g):
                G = (b * 2 + f) * GROUPS + g
                for u in range(2 * TH * FC):
                    e, th, fc = u // (TH * FC), u // FC % TH, u % FC
                    pe.wait_ge(ffn_free[u % 3], 1 + 4 * G + u // 3)
                    nc.tensor.matmul(ffn_bank[u % 3][:, :], w1s[:, 2 * g + e, fc * P:(fc + 1) * P],
                                     fnT[:, th * BANK:(th + 1) * BANK], start=True, stop=True).then_inc(ffn_full[u % 3], 1)

            def experts_out(b, f, g):
                G = (b * 2 + f) * GROUPS + g
                for v in range(2 * TH):
                    e, th = v // TH, v % TH
                    u = 2 * TH * FC + v
                    freed(G, e * TH * FC + th * FC + FC - 1)
                    pe.wait_ge(ffn_free[u % 3], 1 + 4 * G + u // 3)
                    for i in range(QB):
                        tok = slice((th * QB + i) * P, (th * QB + i + 1) * P)
                        for fc in range(FC):
                            last = nc.tensor.matmul(ffn_bank[u % 3][:, i * C:(i + 1) * C], hid[:, e, fc, tok],
                                                    w2s[:, 2 * g + e, fc, :], start=(fc == 0), stop=(fc == FC - 1))
                    last.then_inc(ffn_full[u % 3], 1)

            def attend(b):
                for th in range(TH):
                    side_slot(b, S_QKV + th)
                    nc.tensor.matmul(side_bank[:, :], qkvw[:, :], fnT[:, th * BANK:(th + 1) * BANK],
                                     start=True, stop=True).then_inc(side_full, 1)
                pe.wait_ge(headw_ready, b + 1)
                side_slot(b, S_LGT)
                for tb in range(TB):
                    last = nc.tensor.matmul(side_bank[:, tb * NH:(tb + 1) * NH], wsq[:, tb * P:(tb + 1) * P], hw[:, :],
                                            start=True, stop=True)
                last.then_inc(side_full, 1)
                pe.wait_ge(pi_ready, b + 1)
                for th in range(TH):
                    side_slot(b, S_PIX + th)
                    for i in range(QB):
                        last = nc.tensor.transpose(side_bank[:, i * P:(i + 1) * P], fn[:, th * QB + i, :], ident[:, :])
                    last.then_inc(side_full, 1)
                pe.wait_ge(att_ready, b + 1)
                for th in range(TH):
                    side_slot(b, S_AOUT + th)
                    for i in range(QB):
                        tok = slice((th * QB + i) * P, (th * QB + i + 1) * P)
                        last = nc.tensor.matmul(side_bank[:, i * C:(i + 1) * C], att[:, tok], woutw[:, :],
                                                start=True, stop=True)
                    last.then_inc(side_full, 1)

            with pe.Fori(0, NB // 2) as bb:
                for q in range(2):
                    b = bb * 2 + q
                    prep(b, q)
                    pe.wait_ge(prep_free, 1 + PREP_USES * (b + 1))
                    for n in range(NS):
                        spread(b, q, n)
                    project(b, q)
                    for f in range(2):
                        turn_normed(b, (LN_FFN1, LN_FFN2)[f])
                        logits(b, f)
                        for g in range(GROUPS):
                            experts_in(b, f, g)
                            experts_out(b, f, g)
                        if f == 0:
                            turn_normed(b, LN_ATT)
                            attend(b)


_INS = ["x", "ln_g", "ln_b", "in_w", "conv_w", "conv_b", "xproj_w", "dt_w", "dt_b", "A_log", "D", "out_w",
        "Wqkv", "temp", "Wout", "bout", "router_w", "w1", "w2"]


def kernel(**inputs):
    import numpy as np
    import concourse.bacc as bacc
    from concourse.bass_utils import run_bass_kernel_spmd

    names = {("L0_attn_a_" if i < 12 else "L0_attn_b_" if i < 16 else "L0_ffn_") + n: n for i, n in enumerate(_INS)}
    nc = bacc.Bacc("TRN2", target_bir_lowering=False, num_devices=1)
    arrays, args = {}, []
    for full, name in names.items():
        a = np.ascontiguousarray(inputs[full])
        arrays["in_" + name] = a
        args.append(nc.dram_tensor("in_" + name, a.shape, mybir.dt.from_np(a.dtype), kind="ExternalInput").ap())
    shape = inputs["L0_attn_a_x"].shape
    args.append(nc.dram_tensor("out_0", shape, F32, kind="ExternalOutput").ap())
    hybrid_kernel(nc, *args)
    return run_bass_kernel_spmd(nc, [arrays], core_ids=[0]).results[0]["out_0"]
```

```python
from contextlib import ExitStack

import concourse.bass as bass
from concourse import mybir

F32 = mybir.dt.float32
F32R = mybir.dt.float32r
ALU = mybir.AluOpType
ACT = mybir.ActivationFunctionType
X = mybir.AxisListType.X

P = 128
BANK = 512
EPS = 1e-5
NORM2_MIN = 1e-24
PI_EPS = 1e-8
LOWEST = -3.0e38
EXP_LN = "natural_log_exp_and_others"


def hybrid_kernel(nc, x, ln_g, ln_b, in_w, conv_w, conv_b, xproj_w, dt_w, dt_b, A_log, D, out_w,
                  Wqkv, temp, Wout, bout, router_w, w1, w2, out):
    NB, T, C = x.shape
    DI = D.shape[0]
    NS = A_log.shape[0]
    TAPS = conv_w.shape[2]
    PAD = TAPS - 1
    NE, _, FF = w1.shape
    NH = temp.shape[0]
    HD = C // NH
    DH = DI // P
    FC = FF // P
    TB = T // P
    TH = T // BANK
    QB = BANK // P
    NBC = 2 * NS
    PAIRS = NS // 2
    GE = 4
    GROUPS = NE // GE * TH
    assert C == P and DH == 2 and FC == 2 and TH == 2 and NE == 8 and NBC == 32

    ctx = ExitStack()
    with ctx:
        def sb(name, shape, dt=F32):
            return ctx.enter_context(nc.sbuf_tensor(name, shape, dt))

        def ps(name, shape):
            return ctx.enter_context(nc.psum_tensor(name, shape, F32))

        def sem(name):
            return ctx.enter_context(nc.semaphore(name))

        ident = sb("ident", [P, P])
        sel = sb("sel", [4 * NBC, NBC], F32R)
        rev = sb("rev", [P, NE])
        headmask = sb("headmask", [P, NH])
        tempmask = sb("tempmask", [P, NH])
        cols = sb("cols", [P, 4 * DH + 2])
        convb, dtw, dtb, Dcol = (cols[:, i * DH:(i + 1) * DH] for i in range(4))
        gcol, bcol = cols[:, 4 * DH:4 * DH + 1], cols[:, 4 * DH + 1:4 * DH + 2]
        convw = sb("convw", [P, DH, TAPS])
        Aneg = sb("Aneg", [P, NS])
        tapw = sb("tapw", [P, TAPS, DI])
        zw = sb("zw", [P, DI])
        xpw = sb("xpw", [P, DH, 1 + NBC])
        outw = sb("outw", [P, DH, C])
        qkvw = sb("qkvw", [P, C])
        woutw = sb("woutw", [P, C])
        boutr = sb("boutr", [P, C])
        routw = sb("routw", [P, NE])
        w1s = sb("w1s", [P, NE, FF])
        w2s = sb("w2s", [P, NE, FC, C])

        xt = sb("xt", [P, TB, C])
        xa = [sb(f"xa{i}", [P, TB, C]) for i in range(2)]
        xnT = sb("xnT", [P, PAD + T])
        ypost = [sb(f"ypost{i}", [P, DH, T]) for i in range(2)]
        zs = [sb(f"zs{i}", [P, DH, T]) for i in range(2)]
        delta = [sb(f"delta{i}", [P, DH, T]) for i in range(2)]
        du = [sb(f"du{i}", [P, DH, T]) for i in range(2)]
        bcs = sb("bcs", [4 * NBC, T], F32R)
        soft = sb("soft", [P, DH, T])
        xn = soft[:, 0, :].rearrange("p (b c) -> p b c", c=C)
        dA = [sb(f"dA{i}", [P, DH, T]) for i in range(4)]
        hs = [sb(f"hs{i}", [P, DH, T]) for i in range(2)]
        mstat = sb("mstat", [P, TB, 6])
        mmu = sb("mmu", [P, TB])
        mvar = sb("mvar", [P, TB])
        mq = sb("mq", [P, 2, TB])
        mr = sb("mr", [P, 2, TB])
        mt = sb("mt", [P, 2, TB])

        xr = sb("xr", [P, TB, C])
        fn = sb("fn", [P, TB, C])
        fnT = sb("fnT", [P, T])
        hid = sb("hid", [P, GE, FC, BANK])
        piX = hid[:, 0, :, :].rearrange("p f c -> p (f c)")
        wch = sb("wch", [P, T])
        wsq = sb("wsq", [P, T])
        wout_tmp = [sb(f"wout_tmp{i}", [P, QB, C]) for i in range(2)]
        fstat = sb("fstat", [P, TB, 6])
        fmu = sb("fmu", [P, TB])
        fvar = sb("fvar", [P, TB])
        fq = sb("fq", [P, TB])
        fr = sb("fr", [P, TB])
        ft = sb("ft", [P, TB])
        lg = sb("lg", [P, TB, NE])
        key = sb("key", [P, TB, NE])
        mask0 = sb("mask0", [P, TB, NE])
        mask1 = sb("mask1", [P, TB, NE])
        wt = sb("wt", [P, TB, NE])
        top = sb("top", [P, 2, TB])
        kmax = sb("kmax", [P, TB])
        gap = sb("gap", [P, TB])
        gate = sb("gate", [P, 2, TB])
        nrm = sb("nrm", [P, TH])
        nrmi = sb("nrmi", [P, 1])
        hw = sb("hw", [P, NH])
        pi = sb("pi", [P, TB, NH])
        pmx = sb("pmx", [P, TB])
        psm = sb("psm", [P, TB])
        prc = sb("prc", [P, TB])
        sPi = sb("sPi", [P, TH])
        sPw = sb("sPw", [P, TH])
        acol = sb("acol", [P, 4])

        in_raw = dA[0][:, 0, 0:512].rearrange("p (j c) -> p j c", j=4)
        tap_raw = dA[0][:, 1, :].rearrange("p (k j c) -> p k j c", k=TAPS, j=DH)
        xp_raw = dA[1][0:1 + NBC, 0, 0:DI]
        out_raw = dA[1][:, 1, 0:DI]
        qkv_raw = dA[2][:, 0, 0:C]
        wout_raw = dA[2][:, 0, C:2 * C]
        rout_raw = dA[2][0:NE, 1, 0:C]
        cols_raw = dA[2][0:4 * DH + 2, 1, P:2 * P]
        sel0 = dA[3][:, 0, 0:NBC]
        turns = ([(cols_raw, cols[:, :], 4 * DH + 2)]
                 + [(in_raw[:, DH + j, :], zw[:, j * P:(j + 1) * P], P) for j in range(DH)]
                 + [(tap_raw[:, k, j, :], tapw[:, k, j * P:(j + 1) * P], P)
                    for k in range(TAPS) for j in range(DH)]
                 + [(xp_raw[:, j * P:(j + 1) * P], xpw[:, j, :], 1 + NBC) for j in range(DH)]
                 + [(out_raw[:, j * P:(j + 1) * P], outw[:, j, :], P) for j in range(DH)]
                 + [(qkv_raw, qkvw[:, :], P), (wout_raw, woutw[:, :], P), (rout_raw, routw[:, :], NE)])

        bc_bank = [ps(f"bc_bank{i}", [P, BANK]) for i in range(3)]
        ffn_bank = [ps(f"ffn_bank{i}", [P, BANK]) for i in range(3)]
        prep_bank = ps("prep_bank", [P, BANK])
        side_bank = ps("side_bank", [P, BANK])

        w_loaded = sem("w_loaded")
        const_made = sem("const_made")
        taps_scaled = sem("taps_scaled")
        turned = sem("turned")
        turn_kept = sem("turn_kept")
        setup_act = sem("setup_act")
        setup_dve = sem("setup_dve")
        x_loaded = sem("x_loaded")
        x_used = sem("x_used")
        m_dve = sem("m_dve")
        m_act = sem("m_act")
        m_stats = sem("m_stats")
        m_rsqrt = sem("m_rsqrt")
        xn_ready = sem("xn_ready")
        x0_ready = sem("x0_ready")
        prep_full = sem("prep_full")
        prep_free = sem("prep_free")
        bc_hi = sem("bc_hi")
        bc_split = sem("bc_split")
        soft_ready = sem("soft_ready")
        pool_prep = sem("pool_prep")
        soft_one = sem("soft_one")
        delta_ready = sem("delta_ready")
        du_ready = sem("du_ready")
        yinit = sem("yinit")
        dA_ready = sem("dA_ready")
        scanned = sem("scanned")
        bc_full = sem("bc_full")
        bc_free = sem("bc_free")
        hc_added = sem("hc_added")
        gated = sem("gated")
        side_full = sem("side_full")
        side_free = sem("side_free")
        f_dve = sem("f_dve")
        f_stats = sem("f_stats")
        f_rsqrt = sem("f_rsqrt")
        fn_ready = sem("fn_ready")
        gap_ready = sem("gap_ready")
        gap_exp = sem("gap_exp")
        ffn_full = [sem(f"ffn_full{i}") for i in range(3)]
        ffn_free = [sem(f"ffn_free{i}") for i in range(3)]
        headw_ready = sem("headw_ready")
        lgt_ready = sem("lgt_ready")
        pi_exp = sem("pi_exp")
        pi_ready = sem("pi_ready")
        att_ready = sem("att_ready")
        xr_added = sem("xr_added")
        stored = sem("stored")

        N_LOADS = 18
        M_STEPS, F_STEPS = 10, 126
        BC_USES = 2 * TH * NS
        FFN_USES = 2 * GROUPS * 4
        PREP_USES = 2 + 2 * DH * TH + TH + TH
        SIDE_USES = 19
        ADDS = 2 * GROUPS * GE
        LN_FFN1, LN_ATT, LN_FFN2 = range(3)
        S_OUT, S_TURN = (0, 1), ((2, 4), (6, 8), (15, 17))
        S_ROUTE = ((3, 5), (16, 18))
        S_QKV, S_LGT, S_PIX, S_AOUT = (7, 9), 10, (11, 12), (13, 14)
        assert GROUPS == 4 and TH * FC * GE == 16
        SLOTS = ["H", "G0", "G1", "G2", "G3", "M", "G4", "G5", "G6", "G7"]
        STATES = {"H": [0, 1], "G0": [2, 3], "G1": [4], "G2": [5, 6], "G3": [7], "M": [8, 9, 10],
                  "G4": [11, 12], "G5": [13], "G6": [14], "G7": [15]}
        assert sum(STATES.values(), []) == list(range(NS))
        NOTHING = None

        def steps(eng, step):
            step(0, 0, NOTHING, 1, 2)
            with eng.Fori(0, (NB - 4) // 2) as t:
                for k in range(2):
                    i = t * 2 + (1 + k)
                    step(1 + k, i, i - 1, i + 1, i + 2)
            step(NB - 3, NB - 3, NB - 4, NB - 2, NB - 1)
            step(NB - 2, NB - 2, NB - 3, NB - 1, NOTHING)
            step(NB - 1, NB - 1, NB - 2, NOTHING, NOTHING)
            step(NB, NOTHING, NB - 1, NOTHING, NOTHING)

        block = ctx.enter_context(nc.Block())

        def row(ap, n):
            return ap.rearrange("(a n) -> a n", a=1).to_broadcast([P, n])

        @block.sync
        def _(sp):
            loads = [
                (in_raw, in_w.rearrange("(j p) c -> p j c", p=P)),
                (convw[:, :, :], conv_w.rearrange("(h p) a k -> p h (a k)", p=P)),
                (xp_raw, xproj_w), (out_raw, out_w), (qkv_raw, Wqkv), (wout_raw, Wout), (rout_raw, router_w),
                (cols_raw[0:DH, :], conv_b.rearrange("(h p) -> h p", p=P)),
                (cols_raw[DH:2 * DH, :], dt_w.rearrange("(h p) a -> h (p a)", p=P)),
                (cols_raw[2 * DH:3 * DH, :], dt_b.rearrange("(h p) -> h p", p=P)),
                (cols_raw[3 * DH:4 * DH, :], D.rearrange("(h p) -> h p", p=P)),
                (cols_raw[4 * DH:4 * DH + 1, :], ln_g.rearrange("(a p) -> a p", a=1)),
                (cols_raw[4 * DH + 1:4 * DH + 2, :], ln_b.rearrange("(a p) -> a p", a=1)),
                (Aneg[:, :], row(A_log, NS)), (boutr[:, :], row(bout, C)),
                (tempmask[:, :], row(temp.rearrange("h a -> (h a)"), NH)),
                (w1s[:, :, :], w1.rearrange("e c f -> c e f")),
                (w2s[:, :, :, :], w2.rearrange("e (j f) c -> f e j c", f=P)),
            ]
            assert len(loads) == N_LOADS
            sp.sem_inc(stored, 16)
            sp.dma_start(xt[:, :, :], x[0].rearrange("(b p) c -> p b c", p=P)).then_inc(x_loaded, 16)
            for dst, src in loads:
                sp.dma_start(dst, src).then_inc(w_loaded, 16)

            def load(b):
                sp.wait_ge(x_used, b)
                sp.dma_start(xt[:, :, :], x[b].rearrange("(b p) c -> p b c", p=P)).then_inc(x_loaded, 16)

            def store(b):
                sp.wait_ge(xr_added, 2 + ADDS * (b + 1))
                sp.dma_start(out[b].rearrange("(b p) c -> p b c", p=P), xr[:, :, :]).then_inc(stored, 16)

            load(1)
            load(2)
            with sp.Fori(1, NB - 2) as i:
                load(i + 2)
                store(i - 1)
            for b in range(NB - 3, NB):
                store(b)
            sp.wait_ge(stored, 16 + 16 * NB)

        @block.gpsimd
        def _(pool):
            nc.gpsimd.memset(ident[:, :], 0.0)
            nc.gpsimd.memset(sel0[:, :], 0.0)
            nc.gpsimd.memset(headmask[:, :], 1.0)
            nc.gpsimd.memset(xnT[:, 0:PAD], 0.0)
            nc.gpsimd.iota(rev[:, :], pattern=[[-1, NE]], base=NE, channel_multiplier=0,
                           allow_small_or_imprecise_dtypes=True).then_inc(const_made, 1)
            pool.wait_ge(const_made, 1)
            nc.gpsimd.affine_select(out=ident[:, :], in_=ident[:, :], compare_op=ALU.not_equal, fill=1.0,
                                    base=0, pattern=[[-1, P]], channel_multiplier=1)
            nc.gpsimd.affine_select(out=sel0[:, :], in_=sel0[:, :], compare_op=ALU.not_equal, fill=1.0,
                                    base=0, pattern=[[-1, NBC]], channel_multiplier=1).then_inc(const_made, 1)
            for part in range(1, 4):
                pool.wait_ge(const_made, part + 1)
                nc.gpsimd.affine_select(out=sel0[:, :], in_=sel0[:, :], compare_op=ALU.not_equal, fill=1.0,
                                        base=-part * NBC, pattern=[[-1, NBC]],
                                        channel_multiplier=1).then_inc(const_made, 1)
            nc.gpsimd.affine_select(out=headmask[:, :], in_=headmask[:, :], compare_op=ALU.is_ge, fill=0.0,
                                    base=0, pattern=[[-HD, NH]], channel_multiplier=1).then_inc(const_made, 1)
            pool.wait_ge(const_made, 6)
            nc.gpsimd.affine_select(out=headmask[:, :], in_=headmask[:, :], compare_op=ALU.is_ge, fill=0.0,
                                    base=HD - 1, pattern=[[HD, NH]], channel_multiplier=-1).then_inc(const_made, 1)

            def add_x(b, q):
                pool.wait_ge(x0_ready, b + 1)
                nc.gpsimd.tensor_tensor(xa[q][:, :, :], xa[q][:, :, :], xt[:, :, :], ALU.add).then_inc(x_used, 1)

            def soft_large(b, q):
                pool.wait_ge(soft_ready, b + 1)
                nc.gpsimd.tensor_tensor(delta[q][:, :, :], delta[q][:, :, :], du[q][:, :, :], ALU.add).then_inc(pool_prep, 1)

            def soft_small(b, q):
                pool.wait_ge(soft_one, b + 1)
                nc.gpsimd.tensor_tensor(soft[:, :, :], soft[:, :, :], du[q][:, :, :], ALU.subtract).then_inc(pool_prep, 1)
                pool.wait_ge(pool_prep, 2 * b + 2)
                nc.gpsimd.tensor_tensor(delta[q][:, :, :], delta[q][:, :, :], soft[:, :, :], ALU.add).then_inc(delta_ready, 1)

            def sum_states(b, q, n):
                if n == 0:
                    pool.wait_ge(yinit, b + 1)
                pool.wait_ge(bc_free, 1 + BC_USES * b + 2 * TH * (n + 1))
                pool.wait_ge(hc_added, 1 + NS * b + n)
                nc.gpsimd.tensor_tensor(ypost[q][:, :, :], ypost[q][:, :, :], hs[n % 2][:, :, :], ALU.add).then_inc(hc_added, 1)

            add_x(0, 0)
            soft_large(0, 0)
            soft_small(0, 0)

            def add_expert(b, f, g, v):
                G = (b * 2 + f) * GROUPS + g
                u = GE * FC + v
                rows = slice(g // 2 * QB, (g // 2 + 1) * QB)
                pool.wait_ge(ffn_free[u % 3], 1 + 4 * G + u // 3 + 1)
                pool.wait_ge(xr_added, 2 + GE * G + v)
                nc.gpsimd.tensor_tensor(xr[:, rows, :], xr[:, rows, :], wout_tmp[v % 2][:, :, :], ALU.add).then_inc(xr_added, 1)

            def step(k, scan, ffn, proj, norm):
                q = k % 2
                for slot in SLOTS:
                    here = list(STATES[slot]) if scan is not NOTHING else []

                    def next_state():
                        if here:
                            sum_states(scan, q, here.pop(0))

                    if slot[0] == "G" and ffn is not NOTHING:
                        f, g = int(slot[1]) // GROUPS, int(slot[1]) % GROUPS
                        if len(STATES[slot]) == 2:
                            next_state()
                        add_expert(ffn, f, g, 0)
                        add_expert(ffn, f, g, 1)
                        next_state()
                        add_expert(ffn, f, g, 2)
                        add_expert(ffn, f, g, 3)
                    while here:
                        next_state()
                    if proj is not NOTHING:
                        if slot == "G0":
                            add_x(proj, 1 - q)
                        if slot == "M":
                            soft_large(proj, 1 - q)
                        if slot == "G4":
                            soft_small(proj, 1 - q)

            steps(pool, step)

        @block.scalar
        def _(act):
            act.wait_ge(w_loaded, 16 * N_LOADS)
            nc.scalar.preload_act_table_set(EXP_LN)
            nc.scalar.activation(Aneg[:, :], Aneg[:, :], ACT.Exp).then_inc(setup_act, 1)
            act.wait_ge(setup_act, 1)
            nc.scalar.mul(Aneg[:, :], Aneg[:, :], -1.0).then_inc(setup_act, 1)

            def rsqrt(dst, src, before, done, b, k, per):
                act.wait_ge(before, b + k if per == 1 else b * per + k)
                nc.scalar.activation(dst, src, ACT.Ln).then_inc(done, 1)
                act.wait_ge(done, (b * per + k) * 2 - 1)
                nc.scalar.activation(dst, dst, ACT.Exp, scale=-0.5).then_inc(done, 1)

            def prep_rsqrt(b):
                rsqrt(mr[:, :, :], mq[:, :, :], m_stats, m_rsqrt, b, 1, 1)

            def prep_turned(b):
                for th in range(TH):
                    act.wait_ge(prep_full, PREP_USES * b + th + 1)
                    nc.scalar.activation(xnT[:, PAD + th * BANK:PAD + (th + 1) * BANK], prep_bank[:, :],
                                         ACT.Identity, scale=gcol[:, 0:1], bias=bcol[:, 0:1]).then_inc(prep_free, 1)

            def prep_silu(b, q, uses):
                for k in uses:
                    dh, th = k // TH % DH, k % TH
                    act.wait_ge(prep_full, PREP_USES * b + TH + k + 1)
                    dst = (zs if k < DH * TH else ypost)[q][:, dh, th * BANK:(th + 1) * BANK]
                    if k < DH * TH:
                        nc.scalar.activation(dst, prep_bank[:, :], ACT.Silu).then_inc(prep_free, 1)
                    else:
                        nc.scalar.activation(dst, prep_bank[:, :], ACT.Silu, bias=convb[:, dh:dh + 1]).then_inc(prep_free, 1)

            def prep_high(b, q):
                for th in range(TH):
                    act.wait_ge(prep_full, PREP_USES * b + TH + 2 * DH * TH + th + 1)
                    nc.scalar.activation(bcs[2 * NBC * q:2 * NBC * q + NBC, th * BANK:(th + 1) * BANK], prep_bank[0:NBC, :],
                                         ACT.Copy).then_inc(bc_hi, 1)

            def prep_raw(b, q, th):
                cols = slice(th * BANK, (th + 1) * BANK)
                act.wait_ge(prep_full, PREP_USES * b + 2 * TH + 2 * DH * TH + th + 1)
                for dh in range(DH):
                    nc.scalar.activation(soft[:, dh, cols], prep_bank[:, :], ACT.Abs,
                                         scale=dtw[:, dh:dh + 1], bias=dtb[:, dh:dh + 1])
                    last = nc.scalar.activation(delta[q][:, dh, cols], prep_bank[:, :], ACT.Relu,
                                                scale=dtw[:, dh:dh + 1], bias=dtb[:, dh:dh + 1])
                last.then_inc(prep_free, 1)

            def prep_soft(b, q):
                act.wait_ge(prep_free, 1 + PREP_USES * (b + 1))
                nc.scalar.activation(soft[:, :, :], soft[:, :, :], ACT.Exp, scale=-1.0).then_inc(m_act, 1)
                act.wait_ge(m_act, b + 1)
                nc.scalar.activation(du[q][:, :, :], soft[:, :, :], ACT.Ln, bias=1.0).then_inc(soft_ready, 1)

            def prep_end(b, q):
                act.wait_ge(du_ready, b + 1)
                for dh in range(DH):
                    last = nc.scalar.activation(ypost[q][:, dh, :], ypost[q][:, dh, :], ACT.Copy, scale=Dcol[:, dh:dh + 1])
                last.then_inc(yinit, 1)

            def decay(b, q, n):
                if n == 0:
                    act.wait_ge(delta_ready, b + 1)
                j = NS * b + n
                if not isinstance(j, int) or j >= 4:
                    act.wait_ge(scanned, j - 3)
                nc.scalar.activation(dA[n % 4][:, :, :], delta[q][:, :, :], ACT.Exp, scale=Aneg[:, n:n + 1]).then_inc(dA_ready, 1)

            def norm_rsqrt(b, k, th):
                rows = slice(th * QB, (th + 1) * QB)
                rsqrt(fr[:, rows], fq[:, rows], f_stats, f_rsqrt, b, 2 * k + th + 1, 6)

            def norm_turned(b, k, th):
                act.wait_ge(side_full, SIDE_USES * b + S_TURN[k][th] + 1)
                nc.scalar.activation(fnT[:, th * BANK:(th + 1) * BANK], side_bank[:, :], ACT.Copy).then_inc(side_free, 1)

            def route(b, f, th):
                rows = slice(th * QB, (th + 1) * QB)
                act.wait_ge(gap_ready, 4 * b + 2 * f + th + 1)
                nc.scalar.activation(gap[:, rows], gap[:, rows], ACT.Exp).then_inc(gap_exp, 1)

            def gelus(b, f, g):
                nc.scalar.preload_act_table(ACT.Gelu)
                G = (b * 2 + f) * GROUPS + g
                for u in range(GE * FC):
                    act.wait_ge(ffn_full[u % 3], 4 * G + u // 3 + 1)
                    nc.scalar.activation(hid[:, u // FC, u % FC, :], ffn_bank[u % 3][:, :],
                                         ACT.Gelu).then_inc(ffn_free[u % 3], 1)

            def keep_w(b, th):
                cols = slice(th * BANK, (th + 1) * BANK)
                act.wait_ge(side_full, SIDE_USES * b + S_QKV[th] + 1)
                nc.scalar.activation(wch[:, cols], side_bank[:, :], ACT.Copy)
                nc.scalar.activation(wsq[:, cols], side_bank[:, :], ACT.Square,
                                     accum_out=nrm[:, th:th + 1]).then_inc(side_free, 1)

            def exp_heads(b):
                act.wait_ge(lgt_ready, b + 1)
                nc.scalar.activation(pi[:, :, :], pi[:, :, :], ACT.Exp).then_inc(pi_exp, 1)

            def keep_pi(b):
                for th in range(TH):
                    act.wait_ge(side_full, SIDE_USES * b + S_PIX[th] + 1)
                    nc.scalar.activation(piX[:, th * BANK:(th + 1) * BANK], side_bank[:, :], ACT.Copy,
                                         accum_out=sPi[:, th:th + 1]).then_inc(side_free, 1)

            def exp_ln_set():
                nc.scalar.preload_act_table_set(EXP_LN)

            def silu_set():
                nc.scalar.preload_act_table(ACT.Silu)

            def decays(scan, q, proj, slot):
                if slot == "H":
                    scan, q = proj, 1 - q
                if scan is not NOTHING:
                    for n in STATES[slot]:
                        decay(scan, q, n)

            exp_ln_set()
            prep_rsqrt(0)
            prep_turned(0)
            silu_set()
            prep_silu(0, 0, range(8))
            exp_ln_set()
            prep_high(0, 0)
            prep_raw(0, 0, 0)
            prep_raw(0, 0, 1)
            prep_soft(0, 0)
            prep_rsqrt(1)
            prep_turned(1)
            prep_end(0, 0)
            decays(NOTHING, 1, 0, "H")

            def step(k, scan, ffn, proj, norm):
                q = k % 2
                decays(scan, q, proj, "G0")
                if ffn is not NOTHING:
                    norm_rsqrt(ffn, LN_FFN1, 0)
                if proj is not NOTHING:
                    silu_set()
                    if ffn is not NOTHING:
                        act.wait_ge(gated, TH * (ffn + 1))
                    prep_silu(proj, 1 - q, range(0, 4))
                if ffn is not NOTHING:
                    norm_turned(ffn, LN_FFN1, 0)
                if proj is not NOTHING:
                    prep_silu(proj, 1 - q, range(4, 8))
                exp_ln_set()
                if ffn is not NOTHING:
                    norm_rsqrt(ffn, LN_FFN1, 1)
                    route(ffn, 0, 0)
                for slot, after in zip(SLOTS[1:], SLOTS[2:] + SLOTS[:1]):
                    if slot != "M":
                        if ffn is not NOTHING:
                            g = int(slot[1])
                            gelus(ffn, g // GROUPS, g % GROUPS)
                            exp_ln_set()
                            if slot in ("G0", "G4"):
                                norm_turned(ffn, LN_FFN1 if slot == "G0" else LN_FFN2, 1)
                            if slot == "G3":
                                norm_turned(ffn, LN_ATT, 0)
                        if slot == "G7" and norm is not NOTHING:
                            prep_turned(norm)
                        decays(scan, q, proj, after)
                        if ffn is not NOTHING:
                            if slot in ("G1", "G5"):
                                route(ffn, int(slot == "G5"), 1)
                            if slot == "G2":
                                norm_rsqrt(ffn, LN_ATT, 0)
                            if slot == "G3":
                                keep_w(ffn, 0)
                        if slot == "G5" and norm is not NOTHING:
                            prep_rsqrt(norm)
                        if slot == "G7" and proj is not NOTHING:
                            prep_end(proj, 1 - q)
                        continue
                    if ffn is not NOTHING:
                        norm_rsqrt(ffn, LN_ATT, 1)
                    if proj is not NOTHING:
                        prep_high(proj, 1 - q)
                    if ffn is not NOTHING:
                        norm_turned(ffn, LN_ATT, 1)
                        keep_w(ffn, 1)
                    if proj is not NOTHING:
                        prep_raw(proj, 1 - q, 0)
                    if ffn is not NOTHING:
                        exp_heads(ffn)
                    if proj is not NOTHING:
                        prep_raw(proj, 1 - q, 1)
                    if ffn is not NOTHING:
                        keep_pi(ffn)
                    if proj is not NOTHING:
                        prep_soft(proj, 1 - q)
                    decays(scan, q, proj, after)
                    if ffn is not NOTHING:
                        norm_rsqrt(ffn, LN_FFN2, 0)
                        norm_turned(ffn, LN_FFN2, 0)
                        norm_rsqrt(ffn, LN_FFN2, 1)
                        route(ffn, 1, 0)

            steps(act, step)

        @block.vector
        def _(dve):
            for start in [prep_free, bc_free, side_free, hc_added] + ffn_free:
                nc.vector.sem_inc(start, 1)
            nc.vector.sem_inc(xr_added, 2)
            dve.wait_ge(const_made, 7)
            nc.vector.tensor_copy(sel[:, :], sel0[:, :]).then_inc(setup_dve, 1)
            dve.wait_ge(w_loaded, 16 * N_LOADS)
            nc.vector.tensor_tensor(tempmask[:, :], tempmask[:, :], headmask[:, :], ALU.mult).then_inc(setup_dve, 1)
            for k in range(TAPS):
                for j in range(DH):
                    last = nc.vector.tensor_scalar(tap_raw[:, k, j, :], in_raw[:, j, :], convw[:, j, k:k + 1],
                                                   None, ALU.mult)
            last.then_inc(taps_scaled, 1)
            for i, (_, dst, _) in enumerate(turns):
                dve.wait_ge(turned, i + 1)
                nc.vector.tensor_copy(dst, bc_bank[i % 3][:, 0:dst.shape[-1]]).then_inc(turn_kept, 1)

            class Chain:

                def __init__(self, s, base):
                    self.s, self.base, self.n = s, base, 0

                def __call__(self, ins):
                    self.n += 1
                    ins.then_inc(self.s, 1)
                    dve.wait_ge(self.s, self.base + self.n)

            def newton(step, r, q, t):
                step(nc.vector.tensor_tensor(t, r, r, ALU.mult))
                step(nc.vector.tensor_tensor(t, t, q, ALU.mult))
                step(nc.vector.tensor_scalar(t, t, -0.5, 1.5, ALU.mult, ALU.add))
                step(nc.vector.tensor_tensor(r, r, t, ALU.mult))

            def stats(step, src, stat, mu, var, t):
                for tb in range(src.shape[1]):
                    last = nc.vector.bn_stats(stat[:, tb, :], src[:, tb, :])
                step(last)
                nc.vector.tensor_tensor(mu, stat[:, :, 1], stat[:, :, 4], ALU.add)
                step(nc.vector.tensor_tensor(t, stat[:, :, 1], stat[:, :, 4], ALU.subtract))
                nc.vector.tensor_tensor(var, stat[:, :, 2], stat[:, :, 5], ALU.add)
                step(nc.vector.tensor_tensor(t, t, t, ALU.mult))
                nc.vector.tensor_scalar(mu, mu, 0.5, None, ALU.mult)
                step(nc.vector.scalar_tensor_tensor(out=var, in0=t, scalar=C / 4.0, in1=var, op0=ALU.mult, op1=ALU.add))

            def prep_stats(step, b):
                dve.wait_ge(x_loaded, 16 * (b + 1))
                stats(step, xt, mstat, mmu[:, :], mvar[:, :], mt[:, 0, :])
                step(nc.vector.tensor_scalar(mvar[:, :], mvar[:, :], 1.0 / C, None, ALU.mult))
                step(nc.vector.tensor_scalar(mq[:, 0, :], mvar[:, :], EPS, None, ALU.add))
                nc.vector.scalar_tensor_tensor(out=mq[:, 1, :], in0=mq[:, 0, :], scalar=EPS, in1=mvar[:, :],
                                               op0=ALU.mult, op1=ALU.add).then_inc(m_stats, 1)

            def prep_norm(step, b):
                dve.wait_ge(m_rsqrt, 2 * (b + 1))
                newton(step, mr[:, :, :], mq[:, :, :], mt[:, :, :])
                for tb in range(TB):
                    last = nc.vector.tensor_scalar(xn[:, tb, :], xt[:, tb, :], mmu[:, tb:tb + 1], mr[:, 1, tb:tb + 1],
                                                   ALU.subtract, ALU.mult)
                last.then_inc(xn_ready, 1)

            def prep_x0(b, q):
                for tb in range(TB):
                    last = nc.vector.tensor_scalar(xa[q][:, tb, :], xt[:, tb, :], mmu[:, tb:tb + 1], mr[:, 0, tb:tb + 1],
                                                   ALU.subtract, ALU.mult)
                last.then_inc(x0_ready, 1)

            def prep_split(b, q):
                for th in range(TH):
                    cols = slice(th * BANK, (th + 1) * BANK)
                    dve.wait_ge(bc_hi, TH * b + th + 1)
                    r = 2 * NBC * q
                    nc.vector.tensor_tensor(bcs[r + NBC:r + 2 * NBC, cols], prep_bank[0:NBC, :],
                                            bcs[r:r + NBC, cols].bitcast(F32), ALU.subtract).then_inc(prep_free, 1)

            def prep_one(b, q):
                dve.wait_ge(pool_prep, 2 * b + 1)
                nc.vector.tensor_scalar(du[q][:, :, :], soft[:, :, :], 1.0, -1.0, ALU.add, ALU.add).then_inc(soft_one, 1)

            def prep_du(b, q):
                dve.wait_ge(delta_ready, b + 1)
                nc.vector.tensor_tensor(du[q][:, :, :], delta[q][:, :, :], ypost[q][:, :, :], ALU.mult).then_inc(du_ready, 1)
                dve.wait_ge(du_ready, b + 1)

            def times_b(b, q, n):
                j = NS * b + n
                if not isinstance(j, int) or j >= 2:
                    dve.wait_ge(hc_added, j)
                for th in range(TH):
                    cols = slice(th * BANK, (th + 1) * BANK)
                    u = 2 * TH * n + th
                    dve.wait_ge(bc_full, BC_USES * b + u + 1)
                    nc.vector.tensor_tensor(hs[n % 2][:, :, cols], du[q][:, :, cols],
                                            bc_bank[u % 3][:, :].unsqueeze(1).to_broadcast([P, DH, BANK]),
                                            ALU.mult).then_inc(bc_free, 1)

            def scan(b, q, n):
                j = NS * b + n
                h = hs[n % 2]
                dve.wait_ge(bc_free, 1 + BC_USES * b + 2 * TH * n + TH)
                dve.wait_ge(dA_ready, j + 1)
                for dh in range(DH):
                    last = nc.vector.tensor_tensor_scan(h[:, dh, :], dA[n % 4][:, dh, :], h[:, dh, :], 0.0,
                                                        ALU.mult, ALU.add)
                last.then_inc(scanned, 1)

            def times_c(b, q, n):
                h = hs[n % 2]
                dve.wait_ge(scanned, NS * b + n + 1)
                for th in range(TH):
                    cols = slice(th * BANK, (th + 1) * BANK)
                    u = 2 * TH * n + TH + th
                    dve.wait_ge(bc_full, BC_USES * b + u + 1)
                    nc.vector.tensor_tensor(h[:, :, cols], h[:, :, cols],
                                            bc_bank[u % 3][:, :].unsqueeze(1).to_broadcast([P, DH, BANK]),
                                            ALU.mult).then_inc(bc_free, 1)

            def gate_y(b, q):
                dve.wait_ge(hc_added, 1 + NS * (b + 1))
                for th in range(TH):
                    cols = slice(th * BANK, (th + 1) * BANK)
                    nc.vector.tensor_tensor(ypost[q][:, :, cols], ypost[q][:, :, cols], zs[q][:, :, cols],
                                            ALU.mult).then_inc(gated, 1)

            def half(th):
                return slice(th * QB, (th + 1) * QB)

            def residual(b, q, th):
                dve.wait_ge(stored, 16 + 16 * b)
                dve.wait_ge(side_full, SIDE_USES * b + S_OUT[th] + 1)
                nc.vector.tensor_tensor(xr[:, half(th), :], xa[q][:, half(th), :],
                                        side_bank[:, :].rearrange("p (b c) -> p b c", c=C), ALU.add).then_inc(side_free, 1)
                dve.wait_ge(side_free, 1 + SIDE_USES * b + S_OUT[th] + 1)

            def norm_stats(step, b, k, th):
                rows = half(th)
                stats(step, xr[:, rows, :], fstat[:, rows, :], fmu[:, rows], fvar[:, rows], ft[:, rows])
                nc.vector.tensor_scalar(fq[:, rows], fvar[:, rows], 1.0 / C, EPS, ALU.mult, ALU.add).then_inc(f_stats, 1)

            def norm(step, b, k, th):
                rows = half(th)
                dve.wait_ge(f_rsqrt, 2 * (6 * b + 2 * k + th + 1))
                newton(step, fr[:, rows], fq[:, rows], ft[:, rows])
                for tb in range(th * QB, (th + 1) * QB):
                    last = nc.vector.tensor_scalar(fn[:, tb, :], xr[:, tb, :], fmu[:, tb:tb + 1], fr[:, tb:tb + 1],
                                                   ALU.subtract, ALU.mult)
                last.then_inc(fn_ready, 1)

            def wide(ap):
                return ap.unsqueeze(2).to_broadcast([P, QB, NE])

            def route_top(step, b, f, th):
                r = half(th)
                use = SIDE_USES * b + S_ROUTE[f][th] + 1
                dve.wait_ge(side_full, use)
                nc.vector.tensor_copy(lg[:, r, :], side_bank[:, 0:QB * NE].rearrange("p (b e) -> p b e", e=NE)).then_inc(side_free, 1)
                dve.wait_ge(side_free, 1 + use)
                for i, m in enumerate((mask0, mask1)):
                    step(nc.vector.tensor_reduce(top[:, i, r], lg[:, r, :], X, ALU.max))
                    step(nc.vector.tensor_tensor(key[:, r, :], lg[:, r, :], wide(top[:, i, r]), ALU.is_equal))
                    step(nc.vector.tensor_tensor(key[:, r, :], key[:, r, :],
                                                 rev[:, :].unsqueeze(1).to_broadcast([P, QB, NE]), ALU.mult))
                    step(nc.vector.tensor_reduce(kmax[:, r], key[:, r, :], X, ALU.max))
                    step(nc.vector.tensor_tensor(m[:, r, :], key[:, r, :], wide(kmax[:, r]), ALU.is_equal))
                    if i == 0:
                        step(nc.vector.scalar_tensor_tensor(out=lg[:, r, :], in0=m[:, r, :], scalar=LOWEST,
                                                            in1=lg[:, r, :], op0=ALU.mult, op1=ALU.add))
                nc.vector.tensor_tensor(gap[:, r], top[:, 1, r], top[:, 0, r], ALU.subtract).then_inc(gap_ready, 1)

            def route_gates(step, b, f, th):
                r = half(th)
                dve.wait_ge(gap_exp, 4 * b + 2 * f + th + 1)
                step(nc.vector.tensor_scalar(gate[:, 1, r], gap[:, r], 1.0, None, ALU.add))
                step(nc.vector.reciprocal(gate[:, 0, r], gate[:, 1, r]))
                step(nc.vector.tensor_tensor(gate[:, 1, r], gap[:, r], gate[:, 0, r], ALU.mult))
                nc.vector.tensor_tensor(mask0[:, r, :], mask0[:, r, :], wide(gate[:, 0, r]), ALU.mult)
                step(nc.vector.tensor_tensor(mask1[:, r, :], mask1[:, r, :], wide(gate[:, 1, r]), ALU.mult))
                step(nc.vector.tensor_tensor(wt[:, r, :], mask0[:, r, :], mask1[:, r, :], ALU.add))

            def weigh_expert(b, f, g, v):
                G = (b * 2 + f) * GROUPS + g
                u = GE * FC + v
                rows = half(g // 2)
                e = g % 2 * GE + v
                dve.wait_ge(xr_added, 2 + GE * G + v - 1)
                dve.wait_ge(ffn_full[u % 3], 4 * G + u // 3 + 1)
                nc.vector.tensor_tensor(wout_tmp[v % 2][:, :, :], ffn_bank[u % 3][:, :].rearrange("p (b c) -> p b c", c=C),
                                        wt[:, rows, e:e + 1].to_broadcast([P, QB, C]), ALU.mult).then_inc(ffn_free[u % 3], 1)

            def head_weights(step, b):
                dve.wait_ge(side_free, 1 + SIDE_USES * b + S_QKV[1] + 1)
                step(nc.vector.tensor_tensor(nrmi[:, :], nrm[:, 0:1], nrm[:, 1:2], ALU.add))
                step(nc.vector.tensor_scalar(nrmi[:, :], nrmi[:, :], NORM2_MIN, None, ALU.max))
                step(nc.vector.reciprocal(nrmi[:, :], nrmi[:, :]))
                nc.vector.tensor_scalar(hw[:, :], tempmask[:, :], nrmi[:, 0:1], None, ALU.mult).then_inc(headw_ready, 1)

            def head_max(step, b):
                dve.wait_ge(side_full, SIDE_USES * b + S_LGT + 1)
                nc.vector.tensor_copy(pi[:, :, :], side_bank[:, 0:TB * NH].rearrange("p (b h) -> p b h", h=NH)).then_inc(side_free, 1)
                dve.wait_ge(side_free, 1 + SIDE_USES * b + S_LGT + 1)
                step(nc.vector.tensor_reduce(pmx[:, :], pi[:, :, :], X, ALU.max))
                nc.vector.tensor_tensor(pi[:, :, :], pi[:, :, :], pmx[:, :].unsqueeze(2).to_broadcast([P, TB, NH]),
                                        ALU.subtract).then_inc(lgt_ready, 1)

            def head_softmax(step, b):
                dve.wait_ge(pi_exp, b + 1)
                step(nc.vector.tensor_reduce(psm[:, :], pi[:, :, :], X, ALU.add))
                step(nc.vector.reciprocal(prc[:, :], psm[:, :]))
                nc.vector.tensor_tensor(fn[:, :, :].rearrange("p b (h d) -> p b h d", d=HD),
                                        pi[:, :, :].unsqueeze(3).to_broadcast([P, TB, NH, HD]),
                                        prc[:, :].unsqueeze(2).unsqueeze(3).to_broadcast([P, TB, NH, HD]),
                                        ALU.mult).then_inc(pi_ready, 1)

            def weigh(step, b):
                dve.wait_ge(side_free, 1 + SIDE_USES * b + S_PIX[1] + 1)
                nc.vector.tensor_tensor(acol[:, 0:1], sPi[:, 0:1], sPi[:, 1:2], ALU.add)
                for th in range(TH):
                    cols = slice(th * BANK, (th + 1) * BANK)
                    last = nc.vector.scalar_tensor_tensor(out=wsq[:, cols], in0=piX[:, cols], scalar=1.0, in1=wsq[:, cols],
                                                          op0=ALU.mult, op1=ALU.mult, accum_out=sPw[:, th:th + 1])
                step(last)
                step(nc.vector.tensor_scalar(acol[:, 0:1], acol[:, 0:1], PI_EPS, None, ALU.add))
                step(nc.vector.reciprocal(acol[:, 1:2], acol[:, 0:1]))
                step(nc.vector.tensor_tensor(acol[:, 2:3], sPw[:, 0:1], sPw[:, 1:2], ALU.add))
                step(nc.vector.tensor_tensor(acol[:, 2:3], acol[:, 2:3], acol[:, 1:2], ALU.mult))
                step(nc.vector.tensor_scalar(acol[:, 2:3], acol[:, 2:3], 1.0, -1.0, ALU.add, ALU.mult))
                step(nc.vector.reciprocal(acol[:, 3:4], acol[:, 2:3]))
                for th in range(TH):
                    cols = slice(th * BANK, (th + 1) * BANK)
                    nc.vector.scalar_tensor_tensor(out=wch[:, cols], in0=wch[:, cols], scalar=acol[:, 3:4],
                                                   in1=piX[:, cols], op0=ALU.mult, op1=ALU.mult).then_inc(att_ready, 1)

            def add_bias(step, b):
                dve.wait_ge(fn_ready, 6 * b + 2 * LN_ATT + TH)
                step(nc.vector.tensor_tensor(xr[:, :, :], xr[:, :, :], boutr[:, :].unsqueeze(1).to_broadcast([P, TB, C]),
                                             ALU.add))

            def add_attention(b, th):
                use = SIDE_USES * b + S_AOUT[th] + 1
                dve.wait_ge(side_full, use)
                nc.vector.tensor_tensor(xr[:, half(th), :], xr[:, half(th), :],
                                        side_bank[:, :].rearrange("p (b c) -> p b c", c=C), ALU.add).then_inc(side_free, 1)
                dve.wait_ge(side_free, 1 + use)

            first = Chain(m_dve, 0)
            prep_stats(first, 0)
            prep_norm(first, 0)
            prep_x0(0, 0)
            prep_split(0, 0)
            prep_one(0, 0)
            second = Chain(m_dve, M_STEPS)
            prep_stats(second, 1)
            prep_du(0, 0)
            prep_norm(second, 1)

            def step(k, row, ffn, proj, norm_row):
                q = k % 2
                f_step = Chain(f_dve, ffn * F_STEPS) if ffn is not NOTHING else None
                m_step = Chain(m_dve, norm_row * M_STEPS) if norm_row is not NOTHING else None

                def state(n, *parts):
                    if row is not NOTHING:
                        for part in parts or (times_b, scan, times_c):
                            part(row, q, n)

                s0, s1 = STATES["H"]
                state(s0)
                if ffn is not NOTHING:
                    gate_y(ffn, 1 - q)
                    state(s1, times_b, scan)
                    residual(ffn, 1 - q, 0)
                    norm_stats(f_step, ffn, LN_FFN1, 0)
                    residual(ffn, 1 - q, 1)
                    norm_stats(f_step, ffn, LN_FFN1, 1)
                    norm(f_step, ffn, LN_FFN1, 0)
                    state(s1, times_c)
                    route_top(f_step, ffn, 0, 0)
                    norm(f_step, ffn, LN_FFN1, 1)
                    route_gates(f_step, ffn, 0, 0)
                else:
                    state(s1)
                for slot in SLOTS[1:]:
                    s0, *more = STATES[slot]
                    if slot != "M":
                        if ffn is not NOTHING:
                            g = int(slot[1])
                            f, g = g // GROUPS, g % GROUPS
                            if more:
                                state(s0)
                                if slot == "G2":
                                    dve.wait_ge(xr_added, 2 + ADDS * ffn + 2 * GE)
                                    norm_stats(f_step, ffn, LN_ATT, 0)
                                state(more[0], times_b)
                                weigh_expert(ffn, f, g, 0)
                                state(more[0], scan)
                                weigh_expert(ffn, f, g, 1)
                                state(more[0], times_c)
                                weigh_expert(ffn, f, g, 2)
                                weigh_expert(ffn, f, g, 3)
                            else:
                                state(s0, times_b, scan)
                                weigh_expert(ffn, f, g, 0)
                                weigh_expert(ffn, f, g, 1)
                                state(s0, times_c)
                                weigh_expert(ffn, f, g, 2)
                                weigh_expert(ffn, f, g, 3)
                            if slot in ("G0", "G4"):
                                route_top(f_step, ffn, f, 1)
                            if slot in ("G1", "G5"):
                                route_gates(f_step, ffn, f, 1)
                            if slot == "G2":
                                norm(f_step, ffn, LN_ATT, 0)
                        else:
                            for n in [s0] + more:
                                state(n)
                        if proj is not NOTHING:
                            if slot == "G0":
                                prep_x0(proj, 1 - q)
                            if slot == "G4":
                                prep_one(proj, 1 - q)
                            if slot == "G5":
                                prep_du(proj, 1 - q)
                        if norm_row is not NOTHING:
                            if slot == "G4":
                                prep_stats(m_step, norm_row)
                            if slot == "G6":
                                prep_norm(m_step, norm_row)
                        continue
                    s1, s2 = more
                    if ffn is not NOTHING:
                        dve.wait_ge(xr_added, 2 + ADDS * ffn + 4 * GE)
                        norm_stats(f_step, ffn, LN_ATT, 1)
                    state(s0, times_b)
                    if ffn is not NOTHING:
                        norm(f_step, ffn, LN_ATT, 1)
                    if proj is not NOTHING:
                        prep_split(proj, 1 - q)
                    state(s0, scan, times_c)
                    if ffn is not NOTHING:
                        add_bias(f_step, ffn)
                        head_weights(f_step, ffn)
                    state(s1, times_b)
                    if ffn is not NOTHING:
                        head_max(f_step, ffn)
                    state(s1, scan)
                    if ffn is not NOTHING:
                        head_softmax(f_step, ffn)
                    state(s1, times_c)
                    if ffn is not NOTHING:
                        weigh(f_step, ffn)
                        add_attention(ffn, 0)
                        norm_stats(f_step, ffn, LN_FFN2, 0)
                        add_attention(ffn, 1)
                        state(s2, times_b)
                        norm(f_step, ffn, LN_FFN2, 0)
                        norm_stats(f_step, ffn, LN_FFN2, 1)
                        state(s2, scan)
                        route_top(f_step, ffn, 1, 0)
                        state(s2, times_c)
                        norm(f_step, ffn, LN_FFN2, 1)
                        route_gates(f_step, ffn, 1, 0)
                    else:
                        state(s2)
                assert f_step is None or f_step.n == F_STEPS, f_step.n

            steps(dve, step)

        @block.tensor
        def _(pe):
            pe.wait_ge(const_made, 7)
            pe.wait_ge(w_loaded, 16 * N_LOADS)
            pe.wait_ge(taps_scaled, 1)
            for i, (src, dst, n) in enumerate(turns):
                if i >= 3:
                    pe.wait_ge(turn_kept, i - 2)
                nc.tensor.transpose(bc_bank[i % 3][:, 0:n], src, ident[0:n, 0:n]).then_inc(turned, 1)
            pe.wait_ge(turn_kept, len(turns))
            pe.wait_ge(setup_dve, 2)

            def prep_slot(b, u):
                pe.wait_ge(prep_free, 1 + PREP_USES * b + u)

            def prep_turn(b, th):
                if th == 0:
                    pe.wait_ge(xn_ready, b + 1)
                prep_slot(b, th)
                for i in range(QB):
                    last = nc.tensor.transpose(prep_bank[:, i * P:(i + 1) * P], xn[:, th * QB + i, :], ident[:, :])
                last.then_inc(prep_full, 1)

            def prep_in(b, uses):
                for k in uses:
                    dh, th = k // TH % DH, k % TH
                    prep_slot(b, TH + k)
                    if k < DH * TH:
                        last = nc.tensor.matmul(prep_bank[:, :], zw[:, dh * P:(dh + 1) * P],
                                                xnT[:, PAD + th * BANK:PAD + (th + 1) * BANK], start=True, stop=True)
                    else:
                        for tap in range(TAPS):
                            last = nc.tensor.matmul(prep_bank[:, :], tapw[:, tap, dh * P:(dh + 1) * P],
                                                    xnT[:, th * BANK + tap:th * BANK + tap + BANK],
                                                    start=(tap == 0), stop=(tap == TAPS - 1))
                    last.then_inc(prep_full, 1)

            def prep_x(b, q, k):
                th = k % TH
                prep_slot(b, TH + 2 * DH * TH + k)
                for dh in range(DH):
                    w = xpw[:, dh, 1:1 + NBC] if k < TH else xpw[:, dh, 0:1].to_broadcast([P, P])
                    last = nc.tensor.matmul(prep_bank[0:w.shape[1], :], w, ypost[q][:, dh, th * BANK:(th + 1) * BANK],
                                            start=(dh == 0), stop=(dh == DH - 1))
                last.then_inc(prep_full, 1)

            def spread(b, q, n, k):
                th, j = k % TH, (n if k < TH else NS + n)
                u = 2 * TH * n + k
                if k == 0 and n == 0:
                    pe.wait_ge(prep_free, 1 + PREP_USES * b + 2 * TH + 2 * DH * TH)
                pe.wait_ge(bc_free, 1 + BC_USES * b + max(u - 2, 0))
                r = slice(2 * NBC * q, 2 * NBC * (q + 1))
                nc.tensor.matmul(bc_bank[u % 3][:, :], sel[r, j:j + 1].to_broadcast([2 * NBC, P]),
                                 bcs[r, th * BANK:(th + 1) * BANK], start=True, stop=True).then_inc(bc_full, 1)

            def side_slot(b, s):
                pe.wait_ge(side_free, 1 + SIDE_USES * b + s)

            def project(b, q, th):
                pe.wait_ge(gated, TH * b + th + 1)
                side_slot(b, S_OUT[th])
                for i in range(QB):
                    tok = slice((th * QB + i) * P, (th * QB + i + 1) * P)
                    for dh in range(DH):
                        last = nc.tensor.matmul(side_bank[:, i * C:(i + 1) * C], ypost[q][:, dh, tok], outw[:, dh, :],
                                                start=(dh == 0), stop=(dh == DH - 1))
                last.then_inc(side_full, 1)

            def turn_normed(b, k, th):
                pe.wait_ge(fn_ready, 6 * b + 2 * k + th + 1)
                side_slot(b, S_TURN[k][th])
                for i in range(QB):
                    last = nc.tensor.transpose(side_bank[:, i * P:(i + 1) * P], fn[:, th * QB + i, :], ident[:, :])
                last.then_inc(side_full, 1)

            def logits(b, f, th):
                side_slot(b, S_ROUTE[f][th])
                for i in range(QB):
                    tok = slice((th * QB + i) * P, (th * QB + i + 1) * P)
                    last = nc.tensor.matmul(side_bank[:, i * NE:(i + 1) * NE], fnT[:, tok], routw[:, :],
                                            start=True, stop=True)
                last.then_inc(side_full, 1)

            def expert_in(b, f, g, u):
                G = (b * 2 + f) * GROUPS + g
                e, fc, th = g % 2 * GE + u // FC, u % FC, g // 2
                pe.wait_ge(ffn_free[u % 3], 1 + 4 * G + u // 3)
                nc.tensor.matmul(ffn_bank[u % 3][:, :], w1s[:, e, fc * P:(fc + 1) * P],
                                 fnT[:, th * BANK:(th + 1) * BANK], start=True, stop=True).then_inc(ffn_full[u % 3], 1)

            def expert_out(b, f, g, v):
                G = (b * 2 + f) * GROUPS + g
                e, u = g % 2 * GE + v, GE * FC + v
                kept = v * FC + FC - 1
                pe.wait_ge(ffn_free[kept % 3], 1 + 4 * G + kept // 3 + 1)
                pe.wait_ge(ffn_free[u % 3], 1 + 4 * G + u // 3)
                for i in range(QB):
                    for fc in range(FC):
                        last = nc.tensor.matmul(ffn_bank[u % 3][:, i * C:(i + 1) * C], hid[:, v, fc, i * P:(i + 1) * P],
                                                w2s[:, e, fc, :], start=(fc == 0), stop=(fc == FC - 1))
                last.then_inc(ffn_full[u % 3], 1)

            def qkv(b, th):
                side_slot(b, S_QKV[th])
                nc.tensor.matmul(side_bank[:, :], qkvw[:, :], fnT[:, th * BANK:(th + 1) * BANK],
                                 start=True, stop=True).then_inc(side_full, 1)

            def head_logits(b):
                pe.wait_ge(headw_ready, b + 1)
                side_slot(b, S_LGT)
                for tb in range(TB):
                    last = nc.tensor.matmul(side_bank[:, tb * NH:(tb + 1) * NH], wsq[:, tb * P:(tb + 1) * P], hw[:, :],
                                            start=True, stop=True)
                last.then_inc(side_full, 1)

            def turn_pi(b):
                pe.wait_ge(pi_ready, b + 1)
                for th in range(TH):
                    side_slot(b, S_PIX[th])
                    for i in range(QB):
                        last = nc.tensor.transpose(side_bank[:, i * P:(i + 1) * P], fn[:, th * QB + i, :], ident[:, :])
                    last.then_inc(side_full, 1)

            def project_out(b, th):
                pe.wait_ge(att_ready, TH * b + th + 1)
                side_slot(b, S_AOUT[th])
                for i in range(QB):
                    tok = slice((th * QB + i) * P, (th * QB + i + 1) * P)
                    last = nc.tensor.matmul(side_bank[:, i * C:(i + 1) * C], wch[:, tok], woutw[:, :],
                                            start=True, stop=True)
                last.then_inc(side_full, 1)

            for th in range(TH):
                prep_turn(0, th)
            prep_slot(0, TH)
            prep_in(0, range(8))
            prep_slot(0, TH + 2 * DH * TH)
            for k in range(2 * TH):
                prep_x(0, 0, k)
            for th in range(TH):
                prep_turn(1, th)

            def step(k, scan, ffn, proj, norm):
                q = k % 2
                q1 = 1 - q
                todo = []

                def states(slot):
                    if scan is not NOTHING:
                        todo.extend((n, part) for n in STATES[slot] for part in range(2 * TH))

                def spreads(count=1):
                    for _ in range(min(count, len(todo))):
                        spread(scan, q, *todo.pop(0))

                states("H")
                spreads(6)
                if ffn is not NOTHING:
                    project(ffn, q1, 0)
                    project(ffn, q1, 1)
                if proj is not NOTHING:
                    prep_slot(proj, TH)
                    prep_in(proj, range(0, 4))
                spreads(2)
                if ffn is not NOTHING:
                    turn_normed(ffn, LN_FFN1, 0)
                if proj is not NOTHING:
                    prep_in(proj, range(4, 5))
                if ffn is not NOTHING:
                    logits(ffn, 0, 0)
                if proj is not NOTHING:
                    prep_in(proj, range(5, 8))
                spreads(len(todo))
                for slot in SLOTS[1:]:
                    states(slot)
                    if slot != "M":
                        per = len(STATES[slot])
                        g = int(slot[1])
                        f, g = g // GROUPS, g % GROUPS
                        for u in range(0, 8, 2):
                            if per == 2 or u % 4 == 0:
                                spreads()
                            if ffn is not NOTHING:
                                expert_in(ffn, f, g, u)
                                expert_in(ffn, f, g, u + 1)
                        if ffn is not NOTHING:
                            if slot in ("G0", "G4"):
                                turn_normed(ffn, LN_FFN2 if f else LN_FFN1, 1)
                            if slot == "G3":
                                turn_normed(ffn, LN_ATT, 0)
                        for v in range(4):
                            if per == 2 or v % 2 == 0:
                                spreads()
                            if slot == "G7" and norm is not NOTHING and v < TH:
                                prep_turn(norm, v)
                            if ffn is not NOTHING:
                                expert_out(ffn, f, g, v)
                                if v == 1 and slot in ("G0", "G4"):
                                    logits(ffn, f, 1)
                                if v == 1 and slot == "G3":
                                    qkv(ffn, 0)
                        continue
                    spreads(2)
                    if proj is not NOTHING:
                        prep_slot(proj, TH + 2 * DH * TH)
                        prep_x(proj, q1, 0)
                        prep_x(proj, q1, 1)
                    if ffn is not NOTHING:
                        turn_normed(ffn, LN_ATT, 1)
                        qkv(ffn, 1)
                    spreads(2)
                    if proj is not NOTHING:
                        prep_x(proj, q1, 2)
                    spreads(2)
                    if ffn is not NOTHING:
                        head_logits(ffn)
                    spreads(1)
                    if proj is not NOTHING:
                        prep_x(proj, q1, 3)
                    if ffn is not NOTHING:
                        turn_pi(ffn)
                    spreads(1)
                    if ffn is not NOTHING:
                        project_out(ffn, 0)
                        project_out(ffn, 1)
                    spreads(2)
                    if ffn is not NOTHING:
                        turn_normed(ffn, LN_FFN2, 0)
                    spreads(1)
                    if ffn is not NOTHING:
                        logits(ffn, 1, 0)
                    spreads(1)
                assert not todo

            steps(pe, step)


_INS = ["x", "ln_g", "ln_b", "in_w", "conv_w", "conv_b", "xproj_w", "dt_w", "dt_b", "A_log", "D", "out_w",
        "Wqkv", "temp", "Wout", "bout", "router_w", "w1", "w2"]


def kernel(**inputs):
    import numpy as np
    import concourse.bacc as bacc
    from concourse.bass_utils import run_bass_kernel_spmd

    names = {("L0_attn_a_" if i < 12 else "L0_attn_b_" if i < 16 else "L0_ffn_") + n: n for i, n in enumerate(_INS)}
    nc = bacc.Bacc("TRN2", target_bir_lowering=False, num_devices=1)
    arrays, args = {}, []
    for full, name in names.items():
        a = np.ascontiguousarray(inputs[full])
        arrays["in_" + name] = a
        args.append(nc.dram_tensor("in_" + name, a.shape, mybir.dt.from_np(a.dtype), kind="ExternalInput").ap())
    shape = inputs["L0_attn_a_x"].shape
    args.append(nc.dram_tensor("out_0", shape, F32, kind="ExternalOutput").ap())
    hybrid_kernel(nc, *args)
    return run_bass_kernel_spmd(nc, [arrays], core_ids=[0]).results[0]["out_0"]
```

```python
from contextlib import ExitStack

import concourse.bass as bass
from concourse import mybir

F32 = mybir.dt.float32
F32R = mybir.dt.float32r
ALU = mybir.AluOpType
ACT = mybir.ActivationFunctionType
X = mybir.AxisListType.X

P = 128
BANK = 512
EPS = 1e-5
NORM2_MIN = 1e-24
PI_EPS = 1e-8
LOWEST = -3.0e38
EXP_LN = "natural_log_exp_and_others"


def hybrid_kernel(nc, x, ln_g, ln_b, in_w, conv_w, conv_b, xproj_w, dt_w, dt_b, A_log, D, out_w,
                  Wqkv, temp, Wout, bout, router_w, w1, w2, out):
    NB, T, C = x.shape
    DI = D.shape[0]
    NS = A_log.shape[0]
    TAPS = conv_w.shape[2]
    PAD = TAPS - 1
    NE, _, FF = w1.shape
    NH = temp.shape[0]
    HD = C // NH
    DH = DI // P
    FC = FF // P
    TB = T // P
    TH = T // BANK
    QB = BANK // P
    NBC = 2 * NS
    PAIRS = NS // 2
    GE = 4
    GROUPS = NE // GE * TH
    assert C == P and DH == 2 and FC == 2 and TH == 2 and NE == 8 and NBC == 32

    ctx = ExitStack()
    with ctx:
        def sb(name, shape, dt=F32):
            return ctx.enter_context(nc.sbuf_tensor(name, shape, dt))

        def ps(name, shape):
            return ctx.enter_context(nc.psum_tensor(name, shape, F32))

        def sem(name):
            return ctx.enter_context(nc.semaphore(name))

        ident = sb("ident", [P, P])
        sel = sb("sel", [4 * NBC, NBC], F32R)
        rev = sb("rev", [P, NE])
        tempmask = sb("tempmask", [P, NH])
        cols = sb("cols", [P, 4 * DH + 2])
        convb, dtw, dtb, Dcol = (cols[:, i * DH:(i + 1) * DH] for i in range(4))
        gcol, bcol = cols[:, 4 * DH:4 * DH + 1], cols[:, 4 * DH + 1:4 * DH + 2]
        convw = sb("convw", [P, DH, TAPS])
        Aneg = sb("Aneg", [P, NS])
        tapw = sb("tapw", [P, TAPS, DI])
        zw = sb("zw", [P, DI])
        xpw = sb("xpw", [P, DH, 1 + NBC])
        outw = sb("outw", [P, DH, C])
        qkvw = sb("qkvw", [P, C])
        woutw = sb("woutw", [P, C])
        boutr = sb("boutr", [P, C])
        routw = sb("routw", [P, NE])
        w1s = sb("w1s", [P, NE, FF])
        w2s = sb("w2s", [P, NE, FC, C])

        xt = sb("xt", [P, TB, C])
        xnT = sb("xnT", [P, PAD + T])
        ypost = [sb(f"ypost{i}", [P, DH, T]) for i in range(2)]
        zs = [sb(f"zs{i}", [P, DH, T]) for i in range(2)]
        delta = [sb(f"delta{i}", [P, DH, T]) for i in range(2)]
        du = [sb(f"du{i}", [P, DH, T]) for i in range(2)]
        bcs = sb("bcs", [4 * NBC, T], F32R)
        soft = sb("soft", [P, DH, T])
        xn = soft[:, 0, :].rearrange("p (b c) -> p b c", c=C)
        dA = [sb(f"dA{i}", [P, DH, T]) for i in range(3)]
        hs = [sb(f"hs{i}", [P, DH, T]) for i in range(2)]
        mstat = sb("mstat", [P, TB, 6])
        mmu = sb("mmu", [P, TB])
        mvar = sb("mvar", [P, TB])
        mq = sb("mq", [P, 2, TB])
        mr = sb("mr", [P, 2, TB])
        mt = sb("mt", [P, 2, TB])
        xscale = [sb(f"xscale{i}", [P, 2, TB]) for i in range(2)]

        xh = sb("xh", [P, TB, C])
        xr = [sb(f"xr{i}", [P, TB, C]) for i in range(2)]
        fn = sb("fn", [P, TB, C])
        fnT = [sb(f"fnT{i}", [P, T]) for i in range(2)]
        hid = sb("hid", [P, GE, FC, BANK])
        piX = sb("piX", [P, T])
        wch = sb("wch", [P, T])
        wsq = sb("wsq", [P, T])
        wout_tmp = [sb(f"wout_tmp{i}", [P, QB, C]) for i in range(2)]
        fstat = sb("fstat", [P, TB, 6])
        fmu = sb("fmu", [P, TB])
        fvar = sb("fvar", [P, TB])
        fq = sb("fq", [P, TB])
        fr = sb("fr", [P, TB])
        ft = sb("ft", [P, TB])
        lg = sb("lg", [P, TB, NE])
        key = sb("key", [P, TB, NE])
        mask1 = sb("mask1", [P, TB, NE])
        wt = [sb(f"wt{i}", [P, TB, NE]) for i in range(2)]
        top = sb("top", [P, 2, TB])
        kmax = sb("kmax", [P, TB])
        gap = sb("gap", [P, TB])
        gate = sb("gate", [P, 2, TB])
        nrm = sb("nrm", [P, TH])
        nrmi = sb("nrmi", [P, 1])
        hw = sb("hw", [P, NH])
        pi = sb("pi", [P, TB, NH])
        pmx = sb("pmx", [P, TB])
        psm = sb("psm", [P, TB])
        prc = sb("prc", [P, TB])
        sums = sb("sums", [P, 2 * TH + 4])
        sPi, sPw, acol = sums[:, 0:TH], sums[:, TH:2 * TH], sums[:, 2 * TH:]

        in_raw = dA[0][:, 0, 0:512].rearrange("p (j c) -> p j c", j=4)
        tap_raw = dA[0][:, 1, :].rearrange("p (k j c) -> p k j c", k=TAPS, j=DH)
        xp_raw = dA[1][0:1 + NBC, 0, 0:DI]
        out_raw = dA[1][:, 1, 0:DI]
        qkv_raw = dA[2][:, 0, 0:C]
        wout_raw = dA[2][:, 0, C:2 * C]
        rout_raw = dA[2][0:NE, 1, 0:C]
        cols_raw = dA[2][0:4 * DH + 2, 1, P:2 * P]
        sel0 = hs[0][:, 0, 0:NBC]
        headmask = hs[0][:, 1, 0:NH]
        turns = ([(cols_raw, cols[:, :], 4 * DH + 2)]
                 + [(in_raw[:, DH + j, :], zw[:, j * P:(j + 1) * P], P) for j in range(DH)]
                 + [(tap_raw[:, k, j, :], tapw[:, k, j * P:(j + 1) * P], P)
                    for k in range(TAPS) for j in range(DH)]
                 + [(xp_raw[:, j * P:(j + 1) * P], xpw[:, j, :], 1 + NBC) for j in range(DH)]
                 + [(out_raw[:, j * P:(j + 1) * P], outw[:, j, :], P) for j in range(DH)]
                 + [(qkv_raw, qkvw[:, :], P), (wout_raw, woutw[:, :], P), (rout_raw, routw[:, :], NE)])

        bc_bank = [ps(f"bc_bank{i}", [P, BANK]) for i in range(3)]
        ffn_bank = [ps(f"ffn_bank{i}", [P, BANK]) for i in range(3)]
        prep_bank = ps("prep_bank", [P, BANK])
        side_bank = ps("side_bank", [P, BANK])

        w_loaded = sem("w_loaded")
        experts_loaded = sem("experts_loaded")
        const_made = sem("const_made")
        taps_scaled = sem("taps_scaled")
        turned = sem("turned")
        turn_kept = sem("turn_kept")
        setup_act = sem("setup_act")
        setup_dve = sem("setup_dve")
        x_loaded = sem("x_loaded")
        xh_loaded = sem("xh_loaded")
        m_dve = sem("m_dve")
        m_act = sem("m_act")
        m_stats = sem("m_stats")
        m_rsqrt = sem("m_rsqrt")
        xn_ready = sem("xn_ready")
        prep_full = sem("prep_full")
        prep_free = sem("prep_free")
        bc_hi = sem("bc_hi")
        soft_ready = sem("soft_ready")
        pool_prep = sem("pool_prep")
        soft_one = sem("soft_one")
        delta_ready = sem("delta_ready")
        du_ready = sem("du_ready")
        yinit = sem("yinit")
        dA_ready = sem("dA_ready")
        scanned = sem("scanned")
        bc_full = sem("bc_full")
        bc_free = sem("bc_free")
        hc_added = sem("hc_added")
        x_scaled = sem("x_scaled")
        gated = sem("gated")
        biased = sem("biased")
        routed = sem("routed")
        side_full = sem("side_full")
        side_free = sem("side_free")
        h_dve = sem("h_dve")
        a_dve = sem("a_dve")
        f_stats = sem("f_stats")
        f_rsqrt = sem("f_rsqrt")
        fn_ready = sem("fn_ready")
        gap_ready = sem("gap_ready")
        gap_exp = sem("gap_exp")
        ffn_full = [sem(f"ffn_full{i}") for i in range(3)]
        ffn_free = [sem(f"ffn_free{i}") for i in range(3)]
        headw_ready = sem("headw_ready")
        lgt_ready = sem("lgt_ready")
        pi_exp = sem("pi_exp")
        pi_ready = sem("pi_ready")
        att_ready = sem("att_ready")
        xr_added = sem("xr_added")
        stored = sem("stored")

        N_LOADS = 16
        M_STEPS, H_STEPS, A_STEPS = 11, 23, 44
        BC_USES = 2 * TH * NS
        PREP_USES = 2 + 2 * DH * TH + TH + TH
        LN_FFN1, LN_ATT, LN_FFN2 = range(3)
        S_OUT, S_TURN = (0, 1), ((2, 3), (5, 7), (14, 15))
        S_ROUTE = (4, 16)
        S_QKV, S_LGT, S_PIX, S_AOUT = (6, 8), 9, (10, 11), (12, 13)
        H_SIDE, A_SIDE = 5, 12
        assert GROUPS == 4 and TH * FC * GE == 16
        SLOTS = ["B0", "B1", "B2", "B3", "A0", "A1", "A2", "A3"]
        assert NS == 2 * len(SLOTS)
        DVE_FIRST = ('A0', 'B1', 'B2')

        NOTHING = None

        def has(i, lag):
            return not isinstance(i, int) or 0 <= i - lag < NB

        def rows(i, lag):
            return min(max(i - lag, 0), NB) if isinstance(i, int) else i - lag

        def side_use(i, s):
            skipped = H_SIDE if s >= H_SIDE and not has(i, 1) else 0
            return rows(i, 1) * H_SIDE + rows(i, 2) * A_SIDE + (s - skipped)

        def group_use(i, f, g):
            return rows(i, 1) * GROUPS + rows(i, 3) * GROUPS + (g + (GROUPS if f == 0 and has(i, 3) else 0))

        def norm_use(i, k):
            return rows(i, 1) + rows(i, 2) * 2 + (0 if k == LN_FFN1 else has(i, 1) + (k - 1))

        def route_use(i, f):
            return rows(i, 1) + rows(i, 2) + (has(i, 1) if f else 0)

        def slot_group(i, slot):
            f = 1 if slot[0] == "B" else 0
            return f, int(slot[1]), has(i, 3 if f else 1)

        def attention_slot(i, s):
            s += 3 * (isinstance(i, int) and i == NB + 1)
            return SLOTS[s] if s < len(SLOTS) else NOTHING

        def turned_tile(i, k):
            return fnT[0 if k == LN_FFN1 or (k == LN_ATT and isinstance(i, int) and i == NB + 1) else 1]

        def steps(eng, step):
            for i in range(3):
                step(i % 2, i)
            with eng.Fori(0, (NB - 4) // 2) as t:
                for k in range(2):
                    step((3 + k) % 2, t * 2 + (3 + k))
            for i in range(NB - 1, NB + 3):
                step(i % 2, i)

        block = ctx.enter_context(nc.Block())

        def half(th):
            return slice(th * QB, (th + 1) * QB)

        def row(ap, n):
            return ap.rearrange("(a n) -> a n", a=1).to_broadcast([P, n])

        @block.sync
        def _(sp):
            loads = [
                (in_raw, in_w.rearrange("(j p) c -> p j c", p=P)),
                (convw[:, :, :], conv_w.rearrange("(h p) a k -> p h (a k)", p=P)),
                (xp_raw, xproj_w), (out_raw, out_w), (qkv_raw, Wqkv), (wout_raw, Wout), (rout_raw, router_w),
                (cols_raw[0:DH, :], conv_b.rearrange("(h p) -> h p", p=P)),
                (cols_raw[DH:2 * DH, :], dt_w.rearrange("(h p) a -> h (p a)", p=P)),
                (cols_raw[2 * DH:3 * DH, :], dt_b.rearrange("(h p) -> h p", p=P)),
                (cols_raw[3 * DH:4 * DH, :], D.rearrange("(h p) -> h p", p=P)),
                (cols_raw[4 * DH:4 * DH + 1, :], ln_g.rearrange("(a p) -> a p", a=1)),
                (cols_raw[4 * DH + 1:4 * DH + 2, :], ln_b.rearrange("(a p) -> a p", a=1)),
                (Aneg[:, :], row(A_log, NS)), (boutr[:, :], row(bout, C)),
                (tempmask[:, :], row(temp.rearrange("h a -> (h a)"), NH)),
            ]
            assert len(loads) == N_LOADS
            sp.sem_inc(stored, 32)
            sp.dma_start(xt[:, :, :], x[0].rearrange("(b p) c -> p b c", p=P)).then_inc(x_loaded, 16)
            for dst, src in loads:
                sp.dma_start(dst, src).then_inc(w_loaded, 16)
            sp.dma_start(w1s[:, :, :], w1.rearrange("e c f -> c e f")).then_inc(experts_loaded, 16)
            sp.dma_start(w2s[:, :, :, :], w2.rearrange("e (j f) c -> f e j c", f=P)).then_inc(experts_loaded, 16)
            sp.dma_start(xh[:, :, :], x[0].rearrange("(b p) c -> p b c", p=P)).then_inc(xh_loaded, 16)

            def load(b):
                sp.wait_ge(xn_ready, b)
                sp.dma_start(xt[:, :, :], x[b].rearrange("(b p) c -> p b c", p=P)).then_inc(x_loaded, 16)

            def load_residual(i):
                sp.wait_ge(xr_added, group_use(i, 0, 2) * GE + (2 + 1))
                sp.dma_start(xh[:, :, :], x[i].rearrange("(b p) c -> p b c", p=P)).then_inc(xh_loaded, 16)

            def store(i, q):
                sp.wait_ge(xr_added, group_use(i, 1, 4) * GE + 2)
                sp.dma_start(out[i - 3].rearrange("(b p) c -> p b c", p=P), xr[1 - q][:, :, :]).then_inc(stored, 16)

            def step(q, i):
                if has(i, -2):
                    load(i + 2)
                if has(i, 3):
                    store(i, q)
                if has(i, 0) and has(i, 1):
                    load_residual(i)

            load(1)
            for i in range(3):
                step(i % 2, i)
            with sp.Fori(0, (NB - 6) // 2) as t:
                for k in range(2):
                    step((3 + k) % 2, t * 2 + (3 + k))
            for i in range(NB - 3, NB + 3):
                step(i % 2, i)
            sp.wait_ge(stored, 32 + 16 * NB)

        @block.gpsimd
        def _(pool):
            nc.gpsimd.memset(ident[:, :], 0.0)
            nc.gpsimd.memset(sel0[:, :], 0.0)
            nc.gpsimd.memset(headmask[:, :], 1.0)
            nc.gpsimd.memset(xnT[:, 0:PAD], 0.0)
            nc.gpsimd.iota(rev[:, :], pattern=[[-1, NE]], base=NE, channel_multiplier=0,
                           allow_small_or_imprecise_dtypes=True).then_inc(const_made, 1)
            pool.wait_ge(const_made, 1)
            nc.gpsimd.affine_select(out=ident[:, :], in_=ident[:, :], compare_op=ALU.not_equal, fill=1.0,
                                    base=0, pattern=[[-1, P]], channel_multiplier=1)
            nc.gpsimd.affine_select(out=sel0[:, :], in_=sel0[:, :], compare_op=ALU.not_equal, fill=1.0,
                                    base=0, pattern=[[-1, NBC]], channel_multiplier=1).then_inc(const_made, 1)
            for part in range(1, 4):
                pool.wait_ge(const_made, part + 1)
                nc.gpsimd.affine_select(out=sel0[:, :], in_=sel0[:, :], compare_op=ALU.not_equal, fill=1.0,
                                        base=-part * NBC, pattern=[[-1, NBC]],
                                        channel_multiplier=1).then_inc(const_made, 1)
            nc.gpsimd.affine_select(out=headmask[:, :], in_=headmask[:, :], compare_op=ALU.is_ge, fill=0.0,
                                    base=0, pattern=[[-HD, NH]], channel_multiplier=1).then_inc(const_made, 1)
            pool.wait_ge(const_made, 6)
            nc.gpsimd.affine_select(out=headmask[:, :], in_=headmask[:, :], compare_op=ALU.is_ge, fill=0.0,
                                    base=HD - 1, pattern=[[HD, NH]], channel_multiplier=-1).then_inc(const_made, 1)

            def soft_large(b, q):
                pool.wait_ge(soft_ready, b + 1)
                nc.gpsimd.tensor_tensor(delta[q][:, :, :], delta[q][:, :, :], du[q][:, :, :], ALU.add).then_inc(pool_prep, 1)

            def soft_small(b, q):
                pool.wait_ge(soft_one, b + 1)
                nc.gpsimd.tensor_tensor(soft[:, :, :], soft[:, :, :], du[q][:, :, :], ALU.subtract).then_inc(pool_prep, 1)
                pool.wait_ge(pool_prep, 2 * b + 2)
                nc.gpsimd.tensor_tensor(delta[q][:, :, :], delta[q][:, :, :], soft[:, :, :], ALU.add).then_inc(delta_ready, 1)

            def sum_states(b, q, n):
                if n == 0:
                    pool.wait_ge(yinit, b + 1)
                pool.wait_ge(bc_free, 1 + BC_USES * b + 2 * TH * (n + 1))
                pool.wait_ge(hc_added, 1 + NS * b + n)
                nc.gpsimd.tensor_tensor(ypost[q][:, :, :], ypost[q][:, :, :], hs[n % 2][:, :, :], ALU.add).then_inc(hc_added, 1)

            def gate_y(i, q):
                pool.wait_ge(hc_added, rows(i, 1) * NS + (NS + 1))
                for th in range(TH):
                    cols = slice(th * BANK, (th + 1) * BANK)
                    nc.gpsimd.tensor_tensor(ypost[q][:, :, cols], ypost[q][:, :, cols], zs[q][:, :, cols],
                                            ALU.mult).then_inc(gated, 1)

            def add_bias(i, xm):
                pool.wait_ge(xr_added, group_use(i, 1, 0) * GE + 2)
                pool.wait_ge(fn_ready, norm_use(i, LN_ATT) + 1)
                nc.gpsimd.tensor_tensor(xm[:, :, :], xm[:, :, :], boutr[:, :].unsqueeze(1).to_broadcast([P, TB, C]),
                                        ALU.add).then_inc(biased, 1)

            def add_expert(i, q, f, g, v):
                G = group_use(i, f, g)
                u = GE * FC + v
                r = half(g // 2)
                pool.wait_ge(ffn_free[u % 3], G * 4 + (u // 3 + 2))
                pool.wait_ge(xr_added, G * GE + (v + 2))
                if f == 0 and g == 0 and v == 0:
                    pool.wait_ge(stored, rows(i, 1) * 16 + 16)
                src = xh if f == 0 and g % 2 == 0 and v == 0 else xr[1 - q]
                nc.gpsimd.tensor_tensor(xr[1 - q][:, r, :], src[:, r, :], wout_tmp[v % 2][:, :, :], ALU.add).then_inc(xr_added, 1)

            def step(q, i):
                for s, slot in enumerate(SLOTS):
                    mslot = attention_slot(i, s)
                    f, g, experts = slot_group(i, slot)
                    if slot == "B0" and has(i, 1):
                        gate_y(i, 1 - q)
                    for j in range(2):
                        if has(i, 0):
                            sum_states(i, q, 2 * s + j)
                        if experts:
                            add_expert(i, q, f, g, 2 * j)
                            add_expert(i, q, f, g, 2 * j + 1)
                    if mslot == "A0" and has(i, 2):
                        add_bias(i, xr[q])
                    if slot == "A1" and has(i, -1):
                        soft_large(i + 1, 1 - q)
                    if slot == "A2" and has(i, -1):
                        soft_small(i + 1, 1 - q)

            steps(pool, step)

        @block.scalar
        def _(act):
            def rsqrt(dst, src, before, done, use):
                act.wait_ge(before, use + 1)
                nc.scalar.activation(dst, src, ACT.Ln).then_inc(done, 1)
                act.wait_ge(done, use * 2 + 1)
                nc.scalar.activation(dst, dst, ACT.Exp, scale=-0.5).then_inc(done, 1)

            def prep_rsqrt(b):
                rsqrt(mr[:, :, :], mq[:, :, :], m_stats, m_rsqrt, b)

            def prep_turned(b, th):
                act.wait_ge(prep_full, PREP_USES * b + th + 1)
                nc.scalar.activation(xnT[:, PAD + th * BANK:PAD + (th + 1) * BANK], prep_bank[:, :],
                                     ACT.Identity, scale=gcol[:, 0:1], bias=bcol[:, 0:1]).then_inc(prep_free, 1)

            def prep_silu(b, q, uses):
                for k in uses:
                    dh, th = k // TH % DH, k % TH
                    act.wait_ge(prep_full, PREP_USES * b + TH + k + 1)
                    dst = (zs if k < DH * TH else ypost)[q][:, dh, th * BANK:(th + 1) * BANK]
                    if k < DH * TH:
                        nc.scalar.activation(dst, prep_bank[:, :], ACT.Silu).then_inc(prep_free, 1)
                    else:
                        nc.scalar.activation(dst, prep_bank[:, :], ACT.Silu, bias=convb[:, dh:dh + 1]).then_inc(prep_free, 1)

            def prep_high(b, q, th):
                act.wait_ge(prep_full, PREP_USES * b + TH + 2 * DH * TH + th + 1)
                nc.scalar.activation(bcs[2 * NBC * q:2 * NBC * q + NBC, th * BANK:(th + 1) * BANK], prep_bank[0:NBC, :],
                                     ACT.Copy).then_inc(bc_hi, 1)

            def prep_raw(b, q, th):
                cols = slice(th * BANK, (th + 1) * BANK)
                act.wait_ge(prep_full, PREP_USES * b + 2 * TH + 2 * DH * TH + th + 1)
                for dh in range(DH):
                    nc.scalar.activation(soft[:, dh, cols], prep_bank[:, :], ACT.Abs,
                                         scale=dtw[:, dh:dh + 1], bias=dtb[:, dh:dh + 1])
                    last = nc.scalar.activation(delta[q][:, dh, cols], prep_bank[:, :], ACT.Relu,
                                                scale=dtw[:, dh:dh + 1], bias=dtb[:, dh:dh + 1])
                last.then_inc(prep_free, 1)

            def prep_soft(b, q):
                act.wait_ge(prep_free, 1 + PREP_USES * (b + 1))
                nc.scalar.activation(soft[:, :, :], soft[:, :, :], ACT.Exp, scale=-1.0).then_inc(m_act, 1)
                act.wait_ge(m_act, b + 1)
                nc.scalar.activation(du[q][:, :, :], soft[:, :, :], ACT.Ln, bias=1.0).then_inc(soft_ready, 1)

            def prep_end(b, q):
                act.wait_ge(du_ready, b + 1)
                for dh in range(DH):
                    last = nc.scalar.activation(ypost[q][:, dh, :], ypost[q][:, dh, :], ACT.Copy, scale=Dcol[:, dh:dh + 1])
                last.then_inc(yinit, 1)

            def decay(b, q, n):
                if n == 0:
                    act.wait_ge(delta_ready, b + 1)
                j = NS * b + n
                ahead = 2 if q == 0 and n < 2 else 3
                if not isinstance(j, int) or j >= ahead:
                    act.wait_ge(scanned, j - (ahead - 1))
                nc.scalar.activation(dA[(n + q) % 3][:, :, :], delta[q][:, :, :], ACT.Exp,
                                     scale=Aneg[:, n:n + 1]).then_inc(dA_ready, 1)

            def norm_rsqrt(i, k):
                rsqrt(fr[:, :], fq[:, :], f_stats, f_rsqrt, norm_use(i, k))

            def norm_turned(i, k, th):
                act.wait_ge(side_full, side_use(i, S_TURN[k][th]) + 1)
                nc.scalar.activation(turned_tile(i, k)[:, th * BANK:(th + 1) * BANK], side_bank[:, :],
                                     ACT.Copy).then_inc(side_free, 1)

            def route(i, f):
                act.wait_ge(gap_ready, route_use(i, f) + 1)
                nc.scalar.activation(gap[:, :], gap[:, :], ACT.Exp).then_inc(gap_exp, 1)

            def scale_x(b, q):
                act.wait_ge(xh_loaded, 16 * (b + 1))
                for tb in range(TB):
                    last = nc.scalar.activation(xh[:, tb, :], xh[:, tb, :], ACT.Identity, scale=xscale[q][:, 0, tb:tb + 1],
                                                bias=xscale[q][:, 1, tb:tb + 1])
                last.then_inc(x_scaled, 1)

            def weigh_expert(i, f, g, v):
                G = group_use(i, f, g)
                u = GE * FC + v
                e = g % 2 * GE + v
                act.wait_ge(routed, route_use(i, 0) + (0 if f else 1))
                act.wait_ge(xr_added, G * GE + (v + 1))
                act.wait_ge(ffn_full[u % 3], G * 4 + (u // 3 + 1))
                for tb in range(QB):
                    last = nc.scalar.activation(wout_tmp[v % 2][:, tb, :], ffn_bank[u % 3][:, tb * C:(tb + 1) * C], ACT.Copy,
                                                scale=wt[f][:, g // 2 * QB + tb, e:e + 1])
                last.then_inc(ffn_free[u % 3], 1)

            def gelu(i, f, g, u):
                act.wait_ge(ffn_full[u % 3], group_use(i, f, g) * 4 + (u // 3 + 1))
                nc.scalar.activation(hid[:, u // FC, u % FC, :], ffn_bank[u % 3][:, :],
                                     ACT.Gelu).then_inc(ffn_free[u % 3], 1)

            def keep_w(i, th):
                cols = slice(th * BANK, (th + 1) * BANK)
                act.wait_ge(side_full, side_use(i, S_QKV[th]) + 1)
                nc.scalar.activation(wch[:, cols], side_bank[:, :], ACT.Copy)
                nc.scalar.activation(wsq[:, cols], side_bank[:, :], ACT.Square,
                                     accum_out=nrm[:, th:th + 1]).then_inc(side_free, 1)

            def exp_heads(i):
                act.wait_ge(lgt_ready, rows(i, 2) + 1)
                nc.scalar.activation(pi[:, :, :], pi[:, :, :], ACT.Exp).then_inc(pi_exp, 1)

            def keep_pi(i, th):
                act.wait_ge(side_full, side_use(i, S_PIX[th]) + 1)
                nc.scalar.activation(piX[:, th * BANK:(th + 1) * BANK], side_bank[:, :], ACT.Copy,
                                     accum_out=sPi[:, th:th + 1]).then_inc(side_free, 1)

            def exp_ln_set():
                nc.scalar.preload_act_table_set(EXP_LN)

            def silu_set():
                nc.scalar.preload_act_table(ACT.Silu)

            exp_ln_set()
            prep_rsqrt(0)
            act.wait_ge(w_loaded, 16 * N_LOADS)
            nc.scalar.activation(Aneg[:, :], Aneg[:, :], ACT.Exp).then_inc(setup_act, 1)
            act.wait_ge(setup_act, 1)
            nc.scalar.mul(Aneg[:, :], Aneg[:, :], -1.0).then_inc(setup_act, 1)
            prep_turned(0, 0)
            prep_turned(0, 1)
            silu_set()
            prep_silu(0, 0, range(8))
            exp_ln_set()
            prep_high(0, 0, 0)
            prep_high(0, 0, 1)
            prep_raw(0, 0, 0)
            prep_raw(0, 0, 1)
            prep_soft(0, 0)
            prep_end(0, 0)
            decay(0, 0, 0)
            decay(0, 0, 1)

            def among(q, i, slot, mslot, pair):
                h, m, p = has(i, 1), has(i, 2), has(i, -1)
                if slot == "B1" and p and pair < TH:
                    prep_turned(i + 1, pair)
                if slot == "B2" and h and pair % 2 == 0:
                    norm_turned(i, LN_FFN1, pair // 2)
                if slot == "A0":
                    if p and pair == 0:
                        prep_high(i + 1, 1 - q, 1)
                if mslot == "A0" and m and pair % 2 == 0:
                    norm_turned(i, LN_ATT, pair // 2)
                if mslot == "A0" and m and pair % 2 == 1:
                    keep_w(i, pair // 2)
                if mslot == "A1" and m and pair in (1, 2):
                    keep_pi(i, pair - 1)

            def step(q, i):
                h, m, p = has(i, 1), has(i, 2), has(i, -1)
                for s, slot in enumerate(SLOTS):
                    mslot = attention_slot(i, s)
                    f, g, experts = slot_group(i, slot)
                    if mslot == "A3" and m:
                        route(i, 1)
                    if experts:
                        nc.scalar.preload_act_table(ACT.Gelu)
                    for pair in range(4):
                        if experts:
                            gelu(i, f, g, 2 * pair)
                            gelu(i, f, g, 2 * pair + 1)
                        among(q, i, slot, mslot, pair)
                    silus = {"B1": (0, 1, 2, 3), "B2": (4, 5), "B3": (6, 7)}.get(slot, ()) if p else ()
                    if slot == "B1" and h:
                        exp_ln_set()
                        norm_rsqrt(i, LN_FFN1)
                    if silus:
                        silu_set()
                        if slot == "B1" and h:
                            act.wait_ge(gated, rows(i, 1) * TH + TH)
                        prep_silu(i + 1, 1 - q, silus[:len(silus) // 2])
                    if experts and slot not in DVE_FIRST:
                        weigh_expert(i, f, g, 0)
                    if silus:
                        prep_silu(i + 1, 1 - q, silus[len(silus) // 2:])
                    exp_ln_set()
                    if slot == "B0" and p:
                        prep_rsqrt(i + 1)
                    if slot == "B3" and h:
                        route(i, 0)
                    if mslot == "B3" and m:
                        norm_rsqrt(i, LN_ATT)
                    if slot == "A1" and p:
                        prep_soft(i + 1, 1 - q)
                    for n in (2 * s + 2, 2 * s + 3):
                        if n < NS and has(i, 0):
                            decay(i, q, n)
                        if n >= NS and p:
                            decay(i + 1, 1 - q, n - NS)
                        if n % 2 == 0:
                            if slot == "A0" and p:
                                prep_raw(i + 1, 1 - q, 0)
                            if mslot == "A2" and m:
                                norm_turned(i, LN_FFN2, 0)
                            if experts:
                                weigh_expert(i, f, g, 2)
                            if mslot == "A2" and m:
                                norm_turned(i, LN_FFN2, 1)
                            if slot == "A0" and p:
                                prep_raw(i + 1, 1 - q, 1)
                    if slot == "B3" and p:
                        prep_high(i + 1, 1 - q, 0)
                    if mslot == "A0" and m:
                        exp_heads(i)
                    if mslot == "A1" and m:
                        norm_rsqrt(i, LN_FFN2)
                    if slot == "A3" and p:
                        prep_end(i + 1, 1 - q)
                    if slot == "A3" and has(i, 0):
                        scale_x(i, q)

            steps(act, step)

        @block.vector
        def _(dve):
            for start in [prep_free, bc_free, side_free, hc_added] + ffn_free:
                nc.vector.sem_inc(start, 1)
            nc.vector.sem_inc(xr_added, 2)
            dve.wait_ge(const_made, 7)
            nc.vector.tensor_copy(sel[:, :], sel0[:, :]).then_inc(setup_dve, 1)
            class Chain:

                def __init__(self, s, base):
                    self.s, self.base, self.n = s, base, 0

                def __call__(self, ins):
                    self.n += 1
                    ins.then_inc(self.s, 1)
                    dve.wait_ge(self.s, self.base + self.n)

            def newton(step, r, q, t):
                step(nc.vector.tensor_tensor(t, r, r, ALU.mult))
                step(nc.vector.tensor_tensor(t, t, q, ALU.mult))
                step(nc.vector.tensor_scalar(t, t, -0.5, 1.5, ALU.mult, ALU.add))
                step(nc.vector.tensor_tensor(r, r, t, ALU.mult))

            def stats(step, src, stat, mu, var, t):
                for tb in range(src.shape[1]):
                    last = nc.vector.bn_stats(stat[:, tb, :], src[:, tb, :])
                step(last)
                nc.vector.tensor_tensor(mu, stat[:, :, 1], stat[:, :, 4], ALU.add)
                step(nc.vector.tensor_tensor(t, stat[:, :, 1], stat[:, :, 4], ALU.subtract))
                nc.vector.tensor_tensor(var, stat[:, :, 2], stat[:, :, 5], ALU.add)
                step(nc.vector.tensor_tensor(t, t, t, ALU.mult))
                nc.vector.tensor_scalar(mu, mu, 0.5, None, ALU.mult)
                step(nc.vector.scalar_tensor_tensor(out=var, in0=t, scalar=C / 4.0, in1=var, op0=ALU.mult, op1=ALU.add))

            def prep_stats(step, b):
                dve.wait_ge(x_loaded, 16 * (b + 1))
                stats(step, xt, mstat, mmu[:, :], mvar[:, :], mt[:, 0, :])
                step(nc.vector.tensor_scalar(mvar[:, :], mvar[:, :], 1.0 / C, None, ALU.mult))
                step(nc.vector.tensor_scalar(mq[:, 0, :], mvar[:, :], EPS, None, ALU.add))
                nc.vector.scalar_tensor_tensor(out=mq[:, 1, :], in0=mq[:, 0, :], scalar=EPS, in1=mvar[:, :],
                                               op0=ALU.mult, op1=ALU.add).then_inc(m_stats, 1)

            def prep_norm(step, b, q):
                dve.wait_ge(m_rsqrt, 2 * (b + 1))
                newton(step, mr[:, :, :], mq[:, :, :], mt[:, :, :])
                nc.vector.tensor_scalar(xscale[q][:, 0, :], mr[:, 0, :], 1.0, None, ALU.add)
                step(nc.vector.scalar_tensor_tensor(out=xscale[q][:, 1, :], in0=mmu[:, :], scalar=-1.0, in1=mr[:, 0, :],
                                                    op0=ALU.mult, op1=ALU.mult))
                for tb in range(TB):
                    last = nc.vector.tensor_scalar(xn[:, tb, :], xt[:, tb, :], mmu[:, tb:tb + 1], mr[:, 1, tb:tb + 1],
                                                   ALU.subtract, ALU.mult)
                last.then_inc(xn_ready, 1)

            def prep_split(b, q, th):
                cols = slice(th * BANK, (th + 1) * BANK)
                dve.wait_ge(bc_hi, TH * b + th + 1)
                r = 2 * NBC * q
                nc.vector.tensor_tensor(bcs[r + NBC:r + 2 * NBC, cols], prep_bank[0:NBC, :],
                                        bcs[r:r + NBC, cols].bitcast(F32), ALU.subtract).then_inc(prep_free, 1)

            def prep_one(b, q):
                dve.wait_ge(pool_prep, 2 * b + 1)
                nc.vector.tensor_scalar(du[q][:, :, :], soft[:, :, :], 1.0, -1.0, ALU.add, ALU.add).then_inc(soft_one, 1)

            def prep_du(b, q):
                dve.wait_ge(delta_ready, b + 1)
                nc.vector.tensor_tensor(du[q][:, :, :], delta[q][:, :, :], ypost[q][:, :, :], ALU.mult).then_inc(du_ready, 1)
                dve.wait_ge(du_ready, b + 1)

            def times_b(b, q, n):
                j = NS * b + n
                if not isinstance(j, int) or j >= 2:
                    dve.wait_ge(hc_added, j)
                for th in range(TH):
                    cols = slice(th * BANK, (th + 1) * BANK)
                    u = 2 * TH * n + th
                    dve.wait_ge(bc_full, BC_USES * b + u + 1)
                    nc.vector.tensor_tensor(hs[n % 2][:, :, cols], du[q][:, :, cols],
                                            bc_bank[u % 3][:, :].unsqueeze(1).to_broadcast([P, DH, BANK]),
                                            ALU.mult).then_inc(bc_free, 1)

            def scan(b, q, n):
                j = NS * b + n
                h = hs[n % 2]
                dve.wait_ge(bc_free, 1 + BC_USES * b + 2 * TH * n + TH)
                dve.wait_ge(dA_ready, j + 1)
                for dh in range(DH):
                    last = nc.vector.tensor_tensor_scan(h[:, dh, :], dA[(n + q) % 3][:, dh, :], h[:, dh, :], 0.0,
                                                        ALU.mult, ALU.add)
                last.then_inc(scanned, 1)

            def times_c(b, q, n):
                h = hs[n % 2]
                dve.wait_ge(scanned, NS * b + n + 1)
                for th in range(TH):
                    cols = slice(th * BANK, (th + 1) * BANK)
                    u = 2 * TH * n + TH + th
                    dve.wait_ge(bc_full, BC_USES * b + u + 1)
                    nc.vector.tensor_tensor(h[:, :, cols], h[:, :, cols],
                                            bc_bank[u % 3][:, :].unsqueeze(1).to_broadcast([P, DH, BANK]),
                                            ALU.mult).then_inc(bc_free, 1)

            def residual(i, th):
                use = side_use(i, S_OUT[th]) + 1
                dve.wait_ge(x_scaled, rows(i, 1) + 1)
                dve.wait_ge(side_full, use)
                nc.vector.tensor_tensor(xh[:, half(th), :], xh[:, half(th), :],
                                        side_bank[:, :].rearrange("p (b c) -> p b c", c=C), ALU.add).then_inc(side_free, 1)
                dve.wait_ge(side_free, use + 1)

            def norm_stats(step, src):
                stats(step, src, fstat, fmu[:, :], fvar[:, :], ft[:, :])
                nc.vector.tensor_scalar(fq[:, :], fvar[:, :], 1.0 / C, EPS, ALU.mult, ALU.add).then_inc(f_stats, 1)

            def norm(step, src, i, k):
                dve.wait_ge(f_rsqrt, norm_use(i, k) * 2 + 2)
                newton(step, fr[:, :], fq[:, :], ft[:, :])
                for tb in range(TB):
                    last = nc.vector.tensor_scalar(fn[:, tb, :], src[:, tb, :], fmu[:, tb:tb + 1], fr[:, tb:tb + 1],
                                                   ALU.subtract, ALU.mult)
                last.then_inc(fn_ready, 1)

            def wide(ap):
                return ap.unsqueeze(2).to_broadcast([P, TB, NE])

            def route_top(step, i, f):
                use = side_use(i, S_ROUTE[f]) + 1
                dve.wait_ge(side_full, use)
                nc.vector.tensor_copy(lg[:, :, :], side_bank[:, 0:TB * NE].rearrange("p (b e) -> p b e", e=NE)).then_inc(side_free, 1)
                dve.wait_ge(side_free, use + 1)
                for place, m in enumerate((wt[f], mask1)):
                    step(nc.vector.tensor_reduce(top[:, place, :], lg[:, :, :], X, ALU.max))
                    step(nc.vector.tensor_tensor(key[:, :, :], lg[:, :, :], wide(top[:, place, :]), ALU.is_equal))
                    step(nc.vector.tensor_tensor(key[:, :, :], key[:, :, :],
                                                 rev[:, :].unsqueeze(1).to_broadcast([P, TB, NE]), ALU.mult))
                    step(nc.vector.tensor_reduce(kmax[:, :], key[:, :, :], X, ALU.max))
                    step(nc.vector.tensor_tensor(m[:, :, :], key[:, :, :], wide(kmax[:, :]), ALU.is_equal))
                    if place == 0:
                        step(nc.vector.scalar_tensor_tensor(out=lg[:, :, :], in0=m[:, :, :], scalar=LOWEST,
                                                            in1=lg[:, :, :], op0=ALU.mult, op1=ALU.add))
                nc.vector.tensor_tensor(gap[:, :], top[:, 1, :], top[:, 0, :], ALU.subtract).then_inc(gap_ready, 1)

            def route_gates(step, i, f):
                dve.wait_ge(gap_exp, route_use(i, f) + 1)
                step(nc.vector.tensor_scalar(gate[:, 1, :], gap[:, :], 1.0, None, ALU.add))
                step(nc.vector.reciprocal(gate[:, 0, :], gate[:, 1, :]))
                step(nc.vector.tensor_tensor(gate[:, 1, :], gap[:, :], gate[:, 0, :], ALU.mult))
                nc.vector.tensor_tensor(wt[f][:, :, :], wt[f][:, :, :], wide(gate[:, 0, :]), ALU.mult)
                step(nc.vector.tensor_tensor(mask1[:, :, :], mask1[:, :, :], wide(gate[:, 1, :]), ALU.mult))
                nc.vector.tensor_tensor(wt[f][:, :, :], wt[f][:, :, :], mask1[:, :, :], ALU.add).then_inc(routed, 1)
                dve.wait_ge(routed, route_use(i, f) + 1)

            def weigh_expert(i, f, g, v):
                G = group_use(i, f, g)
                u = GE * FC + v
                r = half(g // 2)
                e = g % 2 * GE + v
                dve.wait_ge(xr_added, G * GE + (v + 1))
                dve.wait_ge(ffn_full[u % 3], G * 4 + (u // 3 + 1))
                nc.vector.tensor_tensor(wout_tmp[v % 2][:, :, :], ffn_bank[u % 3][:, :].rearrange("p (b c) -> p b c", c=C),
                                        wt[f][:, r, e:e + 1].to_broadcast([P, QB, C]), ALU.mult).then_inc(ffn_free[u % 3], 1)

            def head_weights(step, i):
                dve.wait_ge(side_free, side_use(i, S_QKV[1]) + 2)
                step(nc.vector.tensor_tensor(nrmi[:, :], nrm[:, 0:1], nrm[:, 1:2], ALU.add))
                step(nc.vector.tensor_scalar(nrmi[:, :], nrmi[:, :], NORM2_MIN, None, ALU.max))
                step(nc.vector.reciprocal(nrmi[:, :], nrmi[:, :]))
                nc.vector.tensor_scalar(hw[:, :], tempmask[:, :], nrmi[:, 0:1], None, ALU.mult).then_inc(headw_ready, 1)

            def head_max(step, i):
                dve.wait_ge(side_full, side_use(i, S_LGT) + 1)
                nc.vector.tensor_copy(pi[:, :, :], side_bank[:, 0:TB * NH].rearrange("p (b h) -> p b h", h=NH)).then_inc(side_free, 1)
                dve.wait_ge(side_free, side_use(i, S_LGT) + 2)
                step(nc.vector.tensor_reduce(pmx[:, :], pi[:, :, :], X, ALU.max))
                nc.vector.tensor_tensor(pi[:, :, :], pi[:, :, :], pmx[:, :].unsqueeze(2).to_broadcast([P, TB, NH]),
                                        ALU.subtract).then_inc(lgt_ready, 1)

            def head_softmax(step, i):
                dve.wait_ge(pi_exp, rows(i, 2) + 1)
                step(nc.vector.tensor_reduce(psm[:, :], pi[:, :, :], X, ALU.add))
                step(nc.vector.reciprocal(prc[:, :], psm[:, :]))
                nc.vector.tensor_tensor(fn[:, :, :].rearrange("p b (h d) -> p b h d", d=HD),
                                        pi[:, :, :].unsqueeze(3).to_broadcast([P, TB, NH, HD]),
                                        prc[:, :].unsqueeze(2).unsqueeze(3).to_broadcast([P, TB, NH, HD]),
                                        ALU.mult).then_inc(pi_ready, 1)

            def weigh(step, i):
                dve.wait_ge(side_free, side_use(i, S_PIX[1]) + 2)
                nc.vector.tensor_tensor(acol[:, 0:1], sPi[:, 0:1], sPi[:, 1:2], ALU.add)
                for th in range(TH):
                    cols = slice(th * BANK, (th + 1) * BANK)
                    last = nc.vector.scalar_tensor_tensor(out=wsq[:, cols], in0=piX[:, cols], scalar=1.0, in1=wsq[:, cols],
                                                          op0=ALU.mult, op1=ALU.mult, accum_out=sPw[:, th:th + 1])
                step(last)
                step(nc.vector.tensor_scalar(acol[:, 0:1], acol[:, 0:1], PI_EPS, None, ALU.add))
                step(nc.vector.reciprocal(acol[:, 1:2], acol[:, 0:1]))
                step(nc.vector.tensor_tensor(acol[:, 2:3], sPw[:, 0:1], sPw[:, 1:2], ALU.add))
                step(nc.vector.tensor_tensor(acol[:, 2:3], acol[:, 2:3], acol[:, 1:2], ALU.mult))
                step(nc.vector.tensor_scalar(acol[:, 2:3], acol[:, 2:3], 1.0, -1.0, ALU.add, ALU.mult))
                step(nc.vector.reciprocal(acol[:, 3:4], acol[:, 2:3]))
                for th in range(TH):
                    cols = slice(th * BANK, (th + 1) * BANK)
                    nc.vector.scalar_tensor_tensor(out=wch[:, cols], in0=wch[:, cols], scalar=acol[:, 3:4],
                                                   in1=piX[:, cols], op0=ALU.mult, op1=ALU.mult).then_inc(att_ready, 1)

            def add_attention(i, xm, th):
                use = side_use(i, S_AOUT[th]) + 1
                dve.wait_ge(biased, rows(i, 2) + 1)
                dve.wait_ge(side_full, use)
                nc.vector.tensor_tensor(xm[:, half(th), :], xm[:, half(th), :],
                                        side_bank[:, :].rearrange("p (b c) -> p b c", c=C), ALU.add).then_inc(side_free, 1)
                dve.wait_ge(side_free, use + 1)

            first = Chain(m_dve, 0)
            prep_stats(first, 0)
            prep_norm(first, 0, 0)
            dve.wait_ge(w_loaded, 16 * N_LOADS)
            nc.vector.tensor_tensor(tempmask[:, :], tempmask[:, :], headmask[:, :], ALU.mult).then_inc(setup_dve, 1)
            for k in range(TAPS):
                for j in range(DH):
                    last = nc.vector.tensor_scalar(tap_raw[:, k, j, :], in_raw[:, j, :], convw[:, j, k:k + 1],
                                                   None, ALU.mult)
            last.then_inc(taps_scaled, 1)
            for i, (_, dst, _) in enumerate(turns):
                dve.wait_ge(turned, i + 1)
                nc.vector.tensor_copy(dst, bc_bank[i % 3][:, 0:dst.shape[-1]]).then_inc(turn_kept, 1)

            prep_split(0, 0, 0)
            prep_split(0, 0, 1)
            dve.wait_ge(soft_ready, 1)
            nc.vector.tensor_tensor(delta[0][:, :, :], delta[0][:, :, :], du[0][:, :, :], ALU.add).then_inc(pool_prep, 1)
            prep_one(0, 0)
            dve.wait_ge(soft_one, 1)
            nc.vector.tensor_tensor(soft[:, :, :], soft[:, :, :], du[0][:, :, :], ALU.subtract).then_inc(pool_prep, 1)
            dve.wait_ge(pool_prep, 2)
            nc.vector.tensor_tensor(delta[0][:, :, :], delta[0][:, :, :], soft[:, :, :], ALU.add).then_inc(delta_ready, 1)
            prep_du(0, 0)

            def step(q, i):
                h, m, p = has(i, 1), has(i, 2), has(i, -1)
                q1 = 1 - q
                xm = xr[q]
                p_step = Chain(m_dve, (i + 1) * M_STEPS) if p else None
                h_step = Chain(h_dve, (i - 1) * H_STEPS) if h else None
                a_step = Chain(a_dve, (i - 2) * A_STEPS) if m else None

                def state(part, n):
                    if has(i, 0):
                        part(i, q, n)

                for s, slot in enumerate(SLOTS):
                    mslot = attention_slot(i, s)
                    n0, n1 = 2 * s, 2 * s + 1
                    f, g, experts = slot_group(i, slot)

                    if slot == "B0" and p:
                        prep_stats(p_step, i + 1)
                    if mslot == "B3" and m:
                        dve.wait_ge(xr_added, group_use(i, 1, 0) * GE + 2)
                        norm_stats(a_step, xm)
                    if slot == "A0" and p:
                        prep_split(i + 1, q1, 0)
                    if slot == "B1" and h:
                        residual(i, 1)
                    if mslot == "A3" and m:
                        route_top(a_step, i, 1)
                    state(times_b, n0)
                    if mslot == "A2" and m:
                        norm(a_step, xm, i, LN_FFN2)
                    if slot == "B1" and h:
                        norm_stats(h_step, xh)
                    if slot == "A0" and p:
                        prep_split(i + 1, q1, 1)
                    if mslot == "A1" and m:
                        head_softmax(a_step, i)
                    if slot == "B3" and h:
                        route_top(h_step, i, 0)
                    state(scan, n0)
                    state(times_c, n0)
                    if mslot == "A0" and m:
                        head_weights(a_step, i)
                    if slot == "A2" and p:
                        prep_one(i + 1, q1)
                    if mslot == "A3" and m:
                        route_gates(a_step, i, 1)
                    if mslot == "A1" and m:
                        weigh(a_step, i)
                    state(times_b, n1)
                    if experts and slot in DVE_FIRST:
                        weigh_expert(i, f, g, 0)
                    if slot == "B1" and h:
                        norm(h_step, xh, i, LN_FFN1)
                    state(scan, n1)
                    if slot == "B0" and p:
                        prep_norm(p_step, i + 1, q1)
                    if slot == "B0" and h:
                        residual(i, 0)
                    if mslot == "A0" and m:
                        head_max(a_step, i)
                    if slot == "A3" and p:
                        prep_du(i + 1, q1)
                    if experts:
                        weigh_expert(i, f, g, 1)
                    if slot == "B3" and h:
                        route_gates(h_step, i, 0)
                    if mslot == "A1" and m:
                        add_attention(i, xm, 0)
                    state(times_c, n1)
                    if mslot == "A1" and m:
                        add_attention(i, xm, 1)
                        norm_stats(a_step, xm)
                    if mslot == "B3" and m:
                        norm(a_step, xm, i, LN_ATT)
                    if experts:
                        weigh_expert(i, f, g, 3)
                assert p_step is None or p_step.n == M_STEPS, ("M", p_step.n)
                assert h_step is None or h_step.n == H_STEPS, ("H", h_step.n)
                assert a_step is None or a_step.n == A_STEPS, ("A", a_step.n)

            steps(dve, step)

        @block.tensor
        def _(pe):
            pe.wait_ge(const_made, 7)
            pe.wait_ge(w_loaded, 16 * N_LOADS)
            pe.wait_ge(taps_scaled, 1)
            for i, (src, dst, n) in enumerate(turns):
                if i >= 3:
                    pe.wait_ge(turn_kept, i - 2)
                nc.tensor.transpose(bc_bank[i % 3][:, 0:n], src, ident[0:n, 0:n]).then_inc(turned, 1)
            pe.wait_ge(turn_kept, len(turns))
            pe.wait_ge(setup_dve, 2)

            def prep_slot(b, u):
                pe.wait_ge(prep_free, 1 + PREP_USES * b + u)

            def prep_turn(b, th):
                if th == 0:
                    pe.wait_ge(xn_ready, b + 1)
                prep_slot(b, th)
                for i in range(QB):
                    last = nc.tensor.transpose(prep_bank[:, i * P:(i + 1) * P], xn[:, th * QB + i, :], ident[:, :])
                last.then_inc(prep_full, 1)

            def prep_in(b, uses):
                for k in uses:
                    dh, th = k // TH % DH, k % TH
                    prep_slot(b, TH + k)
                    if k < DH * TH:
                        last = nc.tensor.matmul(prep_bank[:, :], zw[:, dh * P:(dh + 1) * P],
                                                xnT[:, PAD + th * BANK:PAD + (th + 1) * BANK], start=True, stop=True)
                    else:
                        for tap in range(TAPS):
                            last = nc.tensor.matmul(prep_bank[:, :], tapw[:, tap, dh * P:(dh + 1) * P],
                                                    xnT[:, th * BANK + tap:th * BANK + tap + BANK],
                                                    start=(tap == 0), stop=(tap == TAPS - 1))
                    last.then_inc(prep_full, 1)

            def prep_x(b, q, k):
                th = k % TH
                prep_slot(b, TH + 2 * DH * TH + k)
                for dh in range(DH):
                    w = xpw[:, dh, 1:1 + NBC] if k < TH else xpw[:, dh, 0:1].to_broadcast([P, P])
                    last = nc.tensor.matmul(prep_bank[0:w.shape[1], :], w, ypost[q][:, dh, th * BANK:(th + 1) * BANK],
                                            start=(dh == 0), stop=(dh == DH - 1))
                last.then_inc(prep_full, 1)

            def spread(b, q, n, k):
                th, j = k % TH, (n if k < TH else NS + n)
                u = 2 * TH * n + k
                if k == 0 and n == 0:
                    pe.wait_ge(prep_free, 1 + PREP_USES * b + 2 * TH + 2 * DH * TH)
                pe.wait_ge(bc_free, 1 + BC_USES * b + max(u - 2, 0))
                r = slice(2 * NBC * q, 2 * NBC * (q + 1))
                nc.tensor.matmul(bc_bank[u % 3][:, :], sel[r, j:j + 1].to_broadcast([2 * NBC, P]),
                                 bcs[r, th * BANK:(th + 1) * BANK], start=True, stop=True).then_inc(bc_full, 1)

            def side_slot(i, s):
                pe.wait_ge(side_free, side_use(i, s) + 1)

            def project(i, q, th):
                pe.wait_ge(gated, rows(i, 1) * TH + (th + 1))
                side_slot(i, S_OUT[th])
                for tb in range(QB):
                    tok = slice((th * QB + tb) * P, (th * QB + tb + 1) * P)
                    for dh in range(DH):
                        last = nc.tensor.matmul(side_bank[:, tb * C:(tb + 1) * C], ypost[q][:, dh, tok], outw[:, dh, :],
                                                start=(dh == 0), stop=(dh == DH - 1))
                last.then_inc(side_full, 1)

            def turn_normed(i, k, th):
                pe.wait_ge(fn_ready, norm_use(i, k) + 1)
                side_slot(i, S_TURN[k][th])
                for tb in range(QB):
                    last = nc.tensor.transpose(side_bank[:, tb * P:(tb + 1) * P], fn[:, th * QB + tb, :], ident[:, :])
                last.then_inc(side_full, 1)

            def logits(i, f):
                side_slot(i, S_ROUTE[f])
                for tb in range(TB):
                    last = nc.tensor.matmul(side_bank[:, tb * NE:(tb + 1) * NE], fnT[f][:, tb * P:(tb + 1) * P], routw[:, :],
                                            start=True, stop=True)
                last.then_inc(side_full, 1)

            def expert_in(i, f, g, u):
                G = group_use(i, f, g)
                e, fc, th = g % 2 * GE + u // FC, u % FC, g // 2
                pe.wait_ge(ffn_free[u % 3], G * 4 + (u // 3 + 1))
                nc.tensor.matmul(ffn_bank[u % 3][:, :], w1s[:, e, fc * P:(fc + 1) * P],
                                 fnT[f][:, th * BANK:(th + 1) * BANK], start=True, stop=True).then_inc(ffn_full[u % 3], 1)

            def expert_out(i, f, g, v):
                G = group_use(i, f, g)
                e, u = g % 2 * GE + v, GE * FC + v
                kept = v * FC + FC - 1
                pe.wait_ge(ffn_free[kept % 3], G * 4 + (kept // 3 + 2))
                pe.wait_ge(ffn_free[u % 3], G * 4 + (u // 3 + 1))
                for tb in range(QB):
                    for fc in range(FC):
                        last = nc.tensor.matmul(ffn_bank[u % 3][:, tb * C:(tb + 1) * C], hid[:, v, fc, tb * P:(tb + 1) * P],
                                                w2s[:, e, fc, :], start=(fc == 0), stop=(fc == FC - 1))
                last.then_inc(ffn_full[u % 3], 1)

            def qkv(i, th):
                side_slot(i, S_QKV[th])
                nc.tensor.matmul(side_bank[:, :], qkvw[:, :], turned_tile(i, LN_ATT)[:, th * BANK:(th + 1) * BANK],
                                 start=True, stop=True).then_inc(side_full, 1)

            def head_logits(i):
                pe.wait_ge(headw_ready, rows(i, 2) + 1)
                side_slot(i, S_LGT)
                for tb in range(TB):
                    last = nc.tensor.matmul(side_bank[:, tb * NH:(tb + 1) * NH], wsq[:, tb * P:(tb + 1) * P], hw[:, :],
                                            start=True, stop=True)
                last.then_inc(side_full, 1)

            def turn_pi(i, th):
                pe.wait_ge(pi_ready, rows(i, 2) + 1)
                side_slot(i, S_PIX[th])
                for tb in range(QB):
                    last = nc.tensor.transpose(side_bank[:, tb * P:(tb + 1) * P], fn[:, th * QB + tb, :], ident[:, :])
                last.then_inc(side_full, 1)

            def project_out(i, th):
                pe.wait_ge(att_ready, rows(i, 2) * TH + (th + 1))
                side_slot(i, S_AOUT[th])
                for tb in range(QB):
                    tok = slice((th * QB + tb) * P, (th * QB + tb + 1) * P)
                    last = nc.tensor.matmul(side_bank[:, tb * C:(tb + 1) * C], wch[:, tok], woutw[:, :],
                                            start=True, stop=True)
                last.then_inc(side_full, 1)

            for th in range(TH):
                prep_turn(0, th)
            prep_slot(0, TH)
            prep_in(0, range(8))
            prep_slot(0, TH + 2 * DH * TH)
            for k in range(2 * TH):
                prep_x(0, 0, k)
            def chains(q, i, slot, mslot, unit):
                h, m, p = has(i, 1), has(i, 2), has(i, -1)
                q1 = 1 - q
                at = (slot, unit)
                if h:
                    if at in (("B0", 6), ("B0", 7)):
                        project(i, q1, unit - 6)
                    if slot == "B2" and unit in (0, 2):
                        turn_normed(i, LN_FFN1, unit // 2)
                    if at == ("B2", 5):
                        logits(i, 0)
                if m:
                    if mslot == "A0" and unit in (0, 2):
                        turn_normed(i, LN_ATT, unit // 2)
                    if mslot == "A0" and unit in (1, 3):
                        qkv(i, unit // 2)
                    if (mslot, unit) == ("A0", 5):
                        head_logits(i)
                    if mslot == "A1" and unit in (1, 2):
                        turn_pi(i, unit - 1)
                    if mslot == "A1" and unit in (5, 6):
                        project_out(i, unit - 5)
                    if mslot == "A2" and unit in (4, 6):
                        turn_normed(i, LN_FFN2, unit // 2 - 2)
                    if (mslot, unit) == ("A2", 7):
                        logits(i, 1)
                if p:
                    if slot == "B1" and unit < TH:
                        prep_turn(i + 1, unit)
                    if at == ("B1", 3):
                        prep_slot(i + 1, TH)
                    if slot == "B1" and 4 <= unit < 8:
                        prep_in(i + 1, [unit - 4])
                    if slot in ("B2", "B3") and unit in (3, 5):
                        prep_in(i + 1, [(4 if slot == "B2" else 6) + unit // 4])
                    if at == ("B3", 7):
                        prep_slot(i + 1, TH + 2 * DH * TH)
                        prep_x(i + 1, q1, 0)
                    if at in (("A0", 0), ("A0", 4), ("A0", 6)):
                        prep_x(i + 1, q1, 1 if unit == 0 else unit // 2)

            AHEAD = 1

            def step(q, i):
                if isinstance(i, int) and i == 1:
                    pe.wait_ge(experts_loaded, 32)
                for s, slot in enumerate(SLOTS):
                    mslot = attention_slot(i, s)
                    f, g, experts = slot_group(i, slot)
                    for unit in range(8):
                        use = 8 * s + unit + AHEAD
                        if has(i, 0):
                            for use in (range(AHEAD + 1) if use == AHEAD else [use] if use < 2 * TH * NS else []):
                                spread(i, q, use // 4, use % 4)
                        if experts and unit < 4:
                            expert_in(i, f, g, 2 * unit)
                            expert_in(i, f, g, 2 * unit + 1)
                        if experts and unit >= 4:
                            expert_out(i, f, g, unit - 4)
                        chains(q, i, slot, mslot, unit)

            steps(pe, step)


_INS = ["x", "ln_g", "ln_b", "in_w", "conv_w", "conv_b", "xproj_w", "dt_w", "dt_b", "A_log", "D", "out_w",
        "Wqkv", "temp", "Wout", "bout", "router_w", "w1", "w2"]


def kernel(**inputs):
    import numpy as np
    import concourse.bacc as bacc
    from concourse.bass_utils import run_bass_kernel_spmd

    names = {("L0_attn_a_" if i < 12 else "L0_attn_b_" if i < 16 else "L0_ffn_") + n: n for i, n in enumerate(_INS)}
    nc = bacc.Bacc("TRN2", target_bir_lowering=False, num_devices=1)
    arrays, args = {}, []
    for full, name in names.items():
        a = np.ascontiguousarray(inputs[full])
        arrays["in_" + name] = a
        args.append(nc.dram_tensor("in_" + name, a.shape, mybir.dt.from_np(a.dtype), kind="ExternalInput").ap())
    shape = inputs["L0_attn_a_x"].shape
    args.append(nc.dram_tensor("out_0", shape, F32, kind="ExternalOutput").ap())
    hybrid_kernel(nc, *args)
    return run_bass_kernel_spmd(nc, [arrays], core_ids=[0]).results[0]["out_0"]
```
